# Optimizing a Trainium2 kernel written in Bass

```python
import numpy as np
import jax
import jax.numpy as jnp

def _softmax(x, axis=-1):
    return jax.nn.softmax(x, axis=axis)

def _gelu(x):
    return jax.nn.gelu(x, approximate=True)

def _silu(x):
    return jax.nn.silu(x)

def _sigmoid(x):
    return jax.nn.sigmoid(x)

def _layernorm(x, axis=-1, eps=1e-05):
    m = jnp.mean(x, axis=axis, keepdims=True)
    v = jnp.var(x, axis=axis, keepdims=True)
    return (x - m) / jnp.sqrt(v + eps)

def _scatter_add(tgt, idx, src, axis=0):
    return tgt.at[idx].add(src)

def _segment_sum(src, seg, n):
    return jax.ops.segment_sum(src, seg, n)
kernel_name = 'mk_decoder_postln_d1_seqx_r8_c2a7f1'

def setup_inputs(seed: int=0):
    np.random.seed(seed)
    _w = jnp.asarray

    def _rec_inputs():
        import jax
        import jax.numpy as jnp
        _rk = jax.random.key(seed)
        x = 7.22e-05 + 1 * jax.random.normal(jax.random.fold_in(_rk, 1), (16, 128, 128), jnp.float32)
        _lenS = 128 - jax.random.randint(jax.random.fold_in(_rk, 7), (16,), 0, max(1, 128 // 4) + 1, jnp.int32)
        _lenS2 = 128 - jax.random.randint(jax.random.fold_in(_rk, 8), (16,), 0, max(1, 128 // 4) + 1, jnp.int32)
        _ctx_1024P = jax.random.normal(jax.random.fold_in(_rk, 11), (16, 16, 128), jnp.float32)
        _ctx_1024c = jax.random.dirichlet(jax.random.fold_in(_rk, 511), 0.3 * jnp.ones((16,), jnp.float32), (16, 128))
        _ctx_1024t = jnp.einsum('bsk,bkd->bsd', _ctx_1024c, _ctx_1024P)
        _ctx_1024t = _ctx_1024t * jax.lax.rsqrt(jnp.mean(jnp.square(_ctx_1024t)) + 1e-12) * 0.953939
        ctx_1024 = 4.13588e-05 + 0.999923 * (_ctx_1024t + 0.3 * jax.random.normal(jax.random.fold_in(_rk, 611), (16, 128, 128), jnp.float32))
        _validS = jnp.arange(128)[None, :] < _lenS[:, None]
        _validS2 = jnp.arange(128)[None, :] < _lenS2[:, None]
        _causal = jnp.tril(jnp.ones((128, 128), dtype=bool))
        mask_1x1xSxS2_fk0 = jnp.where(jnp.broadcast_to(_validS2[0:1, None, None, :], (1, 1, 128, 128)), 0.0, 1.0).astype(jnp.float32)
        return (x, ctx_1024, mask_1x1xSxS2_fk0)
    x, ctx_1024, mask_1x1xSxS2_fk0 = _rec_inputs()

    def _L0_attn_setup():
        import jax, jax.numpy as jnp
        from jax import lax
        import numpy as np
        B, T, C = (8, 256, 128)
        ATT_SCALE = 1.0
        LN_EPS = 1e-05

        def _layernorm(x, g, b):
            mu = jnp.mean(x, axis=-1, keepdims=True)
            var = jnp.mean(jnp.square(x - mu), axis=-1, keepdims=True)
            return (x - mu) * lax.rsqrt(var + LN_EPS) * g + b

        def _wkv_scan(k, v, td):
            kT = jnp.swapaxes(k, 0, 1)
            vT = jnp.swapaxes(v, 0, 1)

            def step(carry, kv):
                num, den = carry
                kt, vt = kv
                den = den * td + kt
                num = num * td + kt * vt
                return ((num, den), num / (den + 1e-08))
            z = jnp.zeros((k.shape[0], k.shape[2]), dtype=k.dtype)
            _, wkvT = lax.scan(step, (z, z), (kT, vT))
            return jnp.swapaxes(wkvT, 0, 1)

        def _reference_tuple_inner(x, time_decay, time_mix_k, time_mix_v, time_mix_r, Wk, Wv, Wr, Wo, ln_g, ln_b):
            x = _layernorm(x, ln_g, ln_b)
            last_x = jnp.pad(x[:, :-1], ((0, 0), (1, 0), (0, 0)))
            k = (x * time_mix_k + last_x * (1.0 - time_mix_k)) @ Wk.T
            v = (x * time_mix_v + last_x * (1.0 - time_mix_v)) @ Wv.T
            r = (x * time_mix_r + last_x * (1.0 - time_mix_r)) @ Wr.T
            k = k * ATT_SCALE
            td = jnp.exp(time_decay)
            wkv = _wkv_scan(jnp.exp(k), v, td)
            out = jax.nn.sigmoid(r) * wkv @ Wo.T
            new_state = x[:, -1:]
            return (out, new_state)
        key = jax.random.key(seed)
        ks = jax.random.split(key, 10)
        scale = 1.0 / np.sqrt(C)
        x = jax.random.normal(ks[0], (B, T, C), dtype=jnp.float32)
        Wk = jax.random.normal(ks[1], (C, C), dtype=jnp.float32) * scale
        Wv = jax.random.normal(ks[2], (C, C), dtype=jnp.float32) * scale
        Wr = jax.random.normal(ks[3], (C, C), dtype=jnp.float32) * scale
        Wo = jax.random.normal(ks[4], (C, C), dtype=jnp.float32) * scale
        decay_init = jnp.linspace(0.1, 0.45, C, dtype=jnp.float32)
        time_decay = jnp.log(decay_init / (1.0 - decay_init))
        time_mix_k = jax.random.uniform(ks[5], (1, 1, C), dtype=jnp.float32) * 0.375
        time_mix_v = jax.random.uniform(ks[6], (1, 1, C), dtype=jnp.float32) * 0.5
        time_mix_r = jax.random.uniform(ks[7], (1, 1, C), dtype=jnp.float32) * 0.375
        ln_g = jnp.ones((C,), dtype=jnp.float32)
        ln_b = jnp.zeros((C,), dtype=jnp.float32)
        return {'x': x, 'time_decay': time_decay, 'time_mix_k': time_mix_k, 'time_mix_v': time_mix_v, 'time_mix_r': time_mix_r, 'Wk': Wk, 'Wv': Wv, 'Wr': Wr, 'Wo': Wo, 'ln_g': ln_g, 'ln_b': ln_b}
    _L0_attn_all = _L0_attn_setup()
    _L0_attn_in = {k: v for k, v in _L0_attn_all.items() if k in ('time_decay', 'time_mix_k', 'time_mix_v', 'time_mix_r', 'Wk', 'Wv', 'Wr', 'Wo', 'ln_g', 'ln_b')}
    del _L0_attn_all

    def _L0_xattn_setup():
        import jax, jax.numpy as jnp
        import numpy as np
        B, S, D = (4, 256, 128)
        H = 16
        KD = 128
        VD = 128
        key = jax.random.key(seed)
        ks = jax.random.split(key, 8)
        queries = jax.random.normal(ks[0], (B, S, D), dtype=jnp.float32)
        keys_ = jax.random.normal(ks[1], (B, S, D), dtype=jnp.float32)
        values = jax.random.normal(ks[2], (B, S, D), dtype=jnp.float32)
        mask = jnp.tril(jnp.ones((S, S), dtype=jnp.float32))[None, None]
        Wq = jax.random.normal(ks[3], (D, KD), dtype=jnp.float32) / np.sqrt(D)
        Wk = jax.random.normal(ks[4], (D, KD), dtype=jnp.float32) / np.sqrt(D)
        Wv = jax.random.normal(ks[5], (D, VD), dtype=jnp.float32) / np.sqrt(D)
        Wo = jax.random.normal(ks[6], (H * VD // H * H // H * 1 if False else VD, D), dtype=jnp.float32) / np.sqrt(VD)
        bo = jnp.zeros((D,), dtype=jnp.float32)
        return {'queries': queries, 'keys': keys_, 'values': values, 'mask': mask, 'Wq': Wq, 'Wk': Wk, 'Wv': Wv, 'Wo': Wo, 'bo': bo}
    _L0_xattn_all = _L0_xattn_setup()
    _L0_xattn_in = {k: v for k, v in _L0_xattn_all.items() if k in ('Wq', 'Wk', 'Wv', 'Wo', 'bo')}
    del _L0_xattn_all

    def _L0_ffn_setup():
        import jax, jax.numpy as jnp
        import numpy as np
        D_MODEL = 128
        EXPANSION = 4
        D_HIDDEN = D_MODEL * EXPANSION
        NUM_STAGES = int(np.log2(D_HIDDEN))

        def butterfly(y, weights, dim):
            lead = y.shape[:-1]
            for stage in range(weights.shape[0]):
                s = 2 ** stage
                nb = dim // (2 * s)
                yr = y.reshape(*lead, nb, 2, s)
                a = yr[..., 0, :]
                b = yr[..., 1, :]
                w = weights[stage].reshape(nb, s, 2, 2)
                na = w[..., 0, 0] * a + w[..., 0, 1] * b
                nb2 = w[..., 1, 0] * a + w[..., 1, 1] * b
                y = jnp.stack([na, nb2], axis=-2).reshape(*lead, dim)
            return y
        key = jax.random.key(seed)
        ks = jax.random.split(key, 6)
        B, S = (4, 256)
        x = jax.random.normal(ks[0], (B, S, D_MODEL), jnp.float32)
        W_exp = jax.random.normal(ks[1], (D_MODEL, D_HIDDEN), jnp.float32) * 0.02
        b_exp = jnp.zeros((D_HIDDEN,), jnp.float32)
        up_weights = jax.random.normal(ks[2], (NUM_STAGES, D_HIDDEN // 2, 2, 2), jnp.float32) * 0.02
        up_bias = jnp.zeros((D_HIDDEN,), jnp.float32)
        down_weights = jax.random.normal(ks[3], (NUM_STAGES, D_HIDDEN // 2, 2, 2), jnp.float32) * 0.02
        W_con = jax.random.normal(ks[4], (D_HIDDEN, D_MODEL), jnp.float32) * 0.02
        b_con = jnp.zeros((D_MODEL,), jnp.float32)
        down_bias = jnp.zeros((D_MODEL,), jnp.float32)
        return dict(x=x, W_exp=W_exp, b_exp=b_exp, up_weights=up_weights, up_bias=up_bias, down_weights=down_weights, W_con=W_con, b_con=b_con, down_bias=down_bias)
    _L0_ffn_all = _L0_ffn_setup()
    _L0_ffn_in = {k: v for k, v in _L0_ffn_all.items() if k in ('W_exp', 'b_exp', 'up_weights', 'up_bias', 'down_weights', 'W_con', 'b_con', 'down_bias')}
    del _L0_ffn_all
    return {'x': x, 'ctx_1024': ctx_1024, 'mask_1x1xSxS2_fk0': mask_1x1xSxS2_fk0, 'L0_attn_time_decay': _L0_attn_in['time_decay'], 'L0_attn_time_mix_k': _L0_attn_in['time_mix_k'], 'L0_attn_time_mix_v': _L0_attn_in['time_mix_v'], 'L0_attn_time_mix_r': _L0_attn_in['time_mix_r'], 'L0_attn_Wk': _L0_attn_in['Wk'], 'L0_attn_Wv': _L0_attn_in['Wv'], 'L0_attn_Wr': _L0_attn_in['Wr'], 'L0_attn_Wo': _L0_attn_in['Wo'], 'L0_attn_ln_g': _L0_attn_in['ln_g'], 'L0_attn_ln_b': _L0_attn_in['ln_b'], 'L0_xattn_Wq': _L0_xattn_in['Wq'], 'L0_xattn_Wk': _L0_xattn_in['Wk'], 'L0_xattn_Wv': _L0_xattn_in['Wv'], 'L0_xattn_Wo': _L0_xattn_in['Wo'], 'L0_xattn_bo': _L0_xattn_in['bo'], 'L0_ffn_W_exp': _L0_ffn_in['W_exp'], 'L0_ffn_b_exp': _L0_ffn_in['b_exp'], 'L0_ffn_up_weights': _L0_ffn_in['up_weights'], 'L0_ffn_up_bias': _L0_ffn_in['up_bias'], 'L0_ffn_down_weights': _L0_ffn_in['down_weights'], 'L0_ffn_W_con': _L0_ffn_in['W_con'], 'L0_ffn_b_con': _L0_ffn_in['b_con'], 'L0_ffn_down_bias': _L0_ffn_in['down_bias']}

def reference(x, ctx_1024, mask_1x1xSxS2_fk0, L0_attn_time_decay, L0_attn_time_mix_k, L0_attn_time_mix_v, L0_attn_time_mix_r, L0_attn_Wk, L0_attn_Wv, L0_attn_Wr, L0_attn_Wo, L0_attn_ln_g, L0_attn_ln_b, L0_xattn_Wq, L0_xattn_Wk, L0_xattn_Wv, L0_xattn_Wo, L0_xattn_bo, L0_ffn_W_exp, L0_ffn_b_exp, L0_ffn_up_weights, L0_ffn_up_bias, L0_ffn_down_weights, L0_ffn_W_con, L0_ffn_b_con, L0_ffn_down_bias):
    import jax
    import jax.numpy as jnp

    def _L0_attn_ref(x, time_decay, time_mix_k, time_mix_v, time_mix_r, Wk, Wv, Wr, Wo, ln_g, ln_b):
        import jax, jax.numpy as jnp
        from jax import lax
        import numpy as np
        B, T, C = (8, 256, 128)
        ATT_SCALE = 1.0
        LN_EPS = 1e-05

        def _layernorm(x, g, b):
            mu = jnp.mean(x, axis=-1, keepdims=True)
            var = jnp.mean(jnp.square(x - mu), axis=-1, keepdims=True)
            return (x - mu) * lax.rsqrt(var + LN_EPS) * g + b

        def _wkv_scan(k, v, td):
            kT = jnp.swapaxes(k, 0, 1)
            vT = jnp.swapaxes(v, 0, 1)

            def step(carry, kv):
                num, den = carry
                kt, vt = kv
                den = den * td + kt
                num = num * td + kt * vt
                return ((num, den), num / (den + 1e-08))
            z = jnp.zeros((k.shape[0], k.shape[2]), dtype=k.dtype)
            _, wkvT = lax.scan(step, (z, z), (kT, vT))
            return jnp.swapaxes(wkvT, 0, 1)

        def _reference_tuple_inner(x, time_decay, time_mix_k, time_mix_v, time_mix_r, Wk, Wv, Wr, Wo, ln_g, ln_b):
            x = _layernorm(x, ln_g, ln_b)
            last_x = jnp.pad(x[:, :-1], ((0, 0), (1, 0), (0, 0)))
            k = (x * time_mix_k + last_x * (1.0 - time_mix_k)) @ Wk.T
            v = (x * time_mix_v + last_x * (1.0 - time_mix_v)) @ Wv.T
            r = (x * time_mix_r + last_x * (1.0 - time_mix_r)) @ Wr.T
            k = k * ATT_SCALE
            td = jnp.exp(time_decay)
            wkv = _wkv_scan(jnp.exp(k), v, td)
            out = jax.nn.sigmoid(r) * wkv @ Wo.T
            new_state = x[:, -1:]
            return (out, new_state)
        return _reference_tuple_inner(x, time_decay, time_mix_k, time_mix_v, time_mix_r, Wk, Wv, Wr, Wo, ln_g, ln_b)[0]

    def _L0_xattn_ref(queries, keys, values, mask, Wq, Wk, Wv, Wo, bo):
        import jax, jax.numpy as jnp
        import numpy as np
        B, S, D = (4, 256, 128)
        H = 16
        KD = 128
        VD = 128
        b, s, _ = queries.shape
        q = (queries @ Wq).reshape(b, s, H, -1).transpose(0, 2, 1, 3)
        k = (keys @ Wk).reshape(b, s, H, -1).transpose(0, 2, 1, 3)
        v = (values @ Wv).reshape(b, s, H, -1).transpose(0, 2, 1, 3)
        dk = k.shape[-1]
        logits = jnp.einsum('bhqd,bhkd->bhqk', q, k) / jnp.sqrt(jnp.float32(dk))
        logits = logits + (1.0 - mask) * -1000000000.0
        attn = jax.nn.softmax(logits, axis=-1)
        o = jnp.einsum('bhqk,bhkd->bhqd', attn, v)
        o = o.transpose(0, 2, 1, 3).reshape(b, s, H * (VD // H))
        return o @ Wo + bo

    def _L0_ffn_ref(x, W_exp, b_exp, up_weights, up_bias, down_weights, W_con, b_con, down_bias):
        import jax, jax.numpy as jnp
        import numpy as np
        D_MODEL = 128
        EXPANSION = 4
        D_HIDDEN = D_MODEL * EXPANSION
        NUM_STAGES = int(np.log2(D_HIDDEN))

        def butterfly(y, weights, dim):
            lead = y.shape[:-1]
            for stage in range(weights.shape[0]):
                s = 2 ** stage
                nb = dim // (2 * s)
                yr = y.reshape(*lead, nb, 2, s)
                a = yr[..., 0, :]
                b = yr[..., 1, :]
                w = weights[stage].reshape(nb, s, 2, 2)
                na = w[..., 0, 0] * a + w[..., 0, 1] * b
                nb2 = w[..., 1, 0] * a + w[..., 1, 1] * b
                y = jnp.stack([na, nb2], axis=-2).reshape(*lead, dim)
            return y
        h = jnp.einsum('bsd,dh->bsh', x, W_exp) + b_exp
        h = butterfly(h, up_weights, D_HIDDEN)
        h = jax.nn.gelu(h + up_bias, approximate=False)
        h = butterfly(h, down_weights, D_HIDDEN)
        y = jnp.einsum('bsh,hd->bsd', h, W_con) + b_con
        return y + down_bias
    x = _layernorm(x + _L0_attn_ref(x, L0_attn_time_decay, L0_attn_time_mix_k, L0_attn_time_mix_v, L0_attn_time_mix_r, L0_attn_Wk, L0_attn_Wv, L0_attn_Wr, L0_attn_Wo, L0_attn_ln_g, L0_attn_ln_b), axis=-1)
    x = _layernorm(x + _L0_xattn_ref(x, ctx_1024, ctx_1024, mask_1x1xSxS2_fk0, L0_xattn_Wq, L0_xattn_Wk, L0_xattn_Wv, L0_xattn_Wo, L0_xattn_bo), axis=-1)
    x = _layernorm(x + _L0_ffn_ref(x, L0_ffn_W_exp, L0_ffn_b_exp, L0_ffn_up_weights, L0_ffn_up_bias, L0_ffn_down_weights, L0_ffn_W_con, L0_ffn_b_con, L0_ffn_down_bias), axis=-1)
    return x

_drawn_inputs = setup_inputs


def setup_inputs(seed=0):
    import zlib

    import numpy as np

    out = dict(_drawn_inputs(seed))
    spreads = {'L0_attn_ln_g': (1.0, 0.2),
     'L0_attn_ln_b': (0.0, 0.1),
     'L0_xattn_bo': (0.0, 0.1),
     'L0_ffn_b_exp': (0.0, 0.1),
     'L0_ffn_up_bias': (0.0, 0.1),
     'L0_ffn_b_con': (0.0, 0.1),
     'L0_ffn_down_bias': (0.0, 0.1)}
    factors = {'L0_attn_time_mix_r': 3.057}
    for name, (base, spread) in spreads.items():
        noise = np.random.default_rng([zlib.crc32(name.encode()), seed]).standard_normal(out[name].shape)
        drawn = base * np.exp(spread * noise) if base else spread * noise
        out[name] = jnp.asarray(drawn.astype(out[name].dtype))
    for name, factor in factors.items():
        out[name] = (out[name] * factor).astype(out[name].dtype)
    return out
```

```python
from contextlib import ExitStack

import concourse.bass as bass
from concourse import mybir

FP32 = mybir.dt.float32
BF16 = mybir.dt.bfloat16
ALU = mybir.AluOpType
ACT = mybir.ActivationFunctionType
AX = mybir.AxisListType


def decoder_program(nc, x, ctx_t, mask, mask_t, weights, columns, rows, w_exp_t, w_con,
                    up_local, down_local, up_cross, down_cross, out):
    P = 128
    B = x.shape[0]
    C = x.shape[2]
    T = x.shape[1]
    GB = 4
    G = B // GB
    GT = GB * T
    H = 16
    D = C // H
    HQ = 4
    NQ = H // HQ
    VW = D + 1
    STRIP = 32
    FB = w_exp_t.shape[1]
    LOCAL = 7
    EPS = 1e-5
    DEN_EPS = 1e-8
    MASKED = -1000000000.0
    QK_SCALE = float(D) ** -0.5
    PAIRS = [(0, 0), (0, 1), (1, 0), (1, 1), (0, 2), (2, 0)]
    SHIFT_ROW = len(PAIRS) * D
    NS = 3
    SK = 96
    C_DECAY, C_MIXK, C_MIXV, C_MIXR, C_G, C_B, C_UPB = range(7)
    W_K, W_V, W_R, W_O, X_Q, X_K, X_V, X_O = range(8)

    ctx = ExitStack()
    with ctx:
        def sb(name, shape, dt=FP32):
            return ctx.enter_context(nc.sbuf_tensor(name, shape, dt))

        def sem(name):
            return ctx.enter_context(nc.semaphore(name))

        w_sb = sb("w_sb", [P, 8, C])
        col = sb("col", [P, columns.shape[1]])
        row = sb("row", [P, 3, C])
        row_ffn = sb("row_ffn", [P, C])
        ident = sb("ident", [P, P])
        ident_bf = sb("ident_bf", [P, P], BF16)
        one_cell = sb("one_cell", [1, 1])
        one_less = sb("one_less", [P, 3])
        neg_half = sb("neg_half", [P, GB])
        decay = sb("decay", [P, 1])
        decay_row = sb("decay_row", [P, GB, T])
        mask_sb = sb("mask_sb", [P, T])
        mask_t_sb = sb("mask_t_sb", [P, T])
        bias_q = sb("bias_q", [P, T])
        bias_top = sb("bias_top", [P, 1])
        bias_rel = sb("bias_rel", [P, T], BF16)
        bias_k = sb("bias_k", [P, T])

        x_sb = sb("x_sb", [P, B, C])
        xres = sb("xres", [P, B, C])
        ctx_sb = sb("ctx_sb", [P, 2, GT])
        stats = sb("stats", [P, B, 6])
        mv = sb("mv", [P, B, 2])
        rstd = sb("rstd", [P, 4, B])
        nmr = sb("nmr", [P, 4, B])
        z = sb("z", [P, B, C])
        xn = sb("xn", [P, 2, GB, T + 1])
        hidden = sb("hidden", [P, FB, GT])
        w_cur = sb("w_cur", [P, 3, C])
        w_last = sb("w_last", [P, 3, C])
        ek = sb("ek", [P, 2, GT])
        er = sb("er", [P, 2, GT])
        early = sb("early", [P, 5, GT])
        ekv, den, num, gated = early[:, 0, :], early[:, 1, :], early[:, 2, :], early[:, 3:5, :]
        zt = sb("zt", [P, 2, GT])
        part = [sb(f"part_{s}", [P, 2, 3, GT], BF16) for s in "qk"]
        rest = sb("rest", [P, 2, GT])
        stack = [sb(f"stack_{s}", [P, 2, H, GT], BF16) for s in "qk"]
        v_sb = sb("v_sb", [P, B, H, VW])
        probs = sb("probs", [P, 2, H, T])
        top = sb("top", [P, 2, H])
        top_rest = sb("top_rest", [P, H])
        shift = sb("shift", [P, NS, H], BF16)
        shift_t = sb("shift_t", [NS * H, 2, T], BF16)
        o_t = sb("o_t", [P, NQ, T])
        rden = sb("rden", [P, H])
        o_norm = sb("o_norm", [P, H, D])
        o_norm_t = sb("o_norm_t", [P, T])
        wexp_sb = sb("wexp_sb", [P, FB, C + 1])
        wcon_sb = sb("wcon_sb", [P, FB, C])
        n_local = FB * (2 ** (LOCAL + 1) - 2)
        local_w = sb("local_w", [P, 2, 2 * FB * (C + 1)])
        local_m = [[sb(f"local_m{s}{i}", [P, FB * P >> i]) for i in range(2)] for s in range(2)]
        cross_w = sb("cross_w", [P, 2, 16])
        early_flat = early[:].rearrange("p n t -> p (n t)")
        up_rows = early_flat[:, 0:FB * (C + 1)].rearrange("p (f c) -> p f c", f=FB)
        up_cross_m = local_w[:, 0, :].rearrange("p (n f c) -> p n f c", n=2, f=FB)
        down_cross_m = local_w[:, 1, 0:2 * FB * C].rearrange("p (n f c) -> p n f c", n=2, f=FB)
        up_m = early_flat[:, 2 * GT:3 * GT].rearrange("p (f c) -> p f c", f=FB)
        down_m = early_flat[:, 3 * GT:4 * GT].rearrange("p (f c) -> p f c", f=FB)
        up_b = sb("up_b", [P, FB])

        spill = [nc.dram_tensor(f"spill_{s}", [G, 3, P, GT], BF16, kind="Internal").ap() for s in "qk"]

        bank = [ctx.enter_context(nc.psum_tensor(f"bank{i}", [P, 512], FP32)) for i in range(8)]

        w_in, col_in, row_in, mask_in, x_in, ctx_in, ffn_in = [sem(n) for n in (
            "w_in", "col_in", "row_in", "mask_in", "x_in", "ctx_in", "ffn_in")]
        x_in = [sem(f"x_in{g}") for g in range(G)]
        ctx_in = [sem(f"ctx_in{g}") for g in range(G)]
        ident_0 = sem("ident_0")
        ident_1 = sem("ident_1")
        ident_ok = sem("ident_ok")
        const_ok = sem("const_ok")
        dve_const = sem("dve_const")
        decay_ok = sem("decay_ok")
        bias_ok = sem("bias_ok")
        dve_own = sem("dve_own")
        pool_own = sem("pool_own")
        stats_ok = sem("stats_ok")
        rstd_ok = sem("rstd_ok")
        z0_ok = sem("z0_ok")
        t0_ok = sem("t0_ok")
        xn_ok = sem("xn_ok")
        mixw_ok = sem("mixw_ok")
        proj_ok = sem("proj_ok")
        ek_ok = sem("ek_ok")
        er_ok = sem("er_ok")
        ekv_ok = sem("ekv_ok")
        gated_ok = sem("gated_ok")
        y_ok = sem("y_ok")
        res1_ok = sem("res1_ok")
        stats1_ok = sem("stats1_ok")
        rstd1_ok = sem("rstd1_ok")
        z1_ok = sem("z1_ok")
        xres1_ok = sem("xres1_ok")
        t1_ok = sem("t1_ok")
        zt1_ok = sem("zt1_ok")
        q_ok = sem("q_ok")
        q_first = sem("q_first")
        q_rest = sem("q_rest")
        q_second = sem("q_second")
        q_third = sem("q_third")
        kc_ok = sem("kc_ok")
        k_first = sem("k_first")
        k_rest = sem("k_rest")
        k_second = sem("k_second")
        k_third = sem("k_third")
        vc_ok = sem("vc_ok")
        v_ok = sem("v_ok")
        stack_in = [[sem(f"stack_{s}_in{i}") for i in range(2)] for s in "qk"]
        spilled = [[sem(f"spilled_{s}{g}") for g in range(G)] for s in "qk"]
        stack_zero = [sem(f"stack_zero{i}") for i in range(2)]
        stack_filled = [sem(f"stack_{s}_filled") for s in "qk"]
        s1_ok = sem("s1_ok")
        max_ok = sem("max_ok")
        shift_ok = sem("shift_ok")
        shiftt_ok = sem("shiftt_ok")
        shiftt_sb = sem("shiftt_sb")
        shift_in = [sem(f"shift_in{i}") for i in range(2)]
        s2_ok = sem("s2_ok")
        added_ok = sem("added_ok")
        exp_ok = sem("exp_ok")
        av_ok = sem("av_ok")
        ot_ok = sem("ot_ok")
        ox_ok = sem("ox_ok")
        rden_ok = sem("rden_ok")
        norm_ok = sem("norm_ok")
        nt_ok = sem("nt_ok")
        ntsb_ok = sem("ntsb_ok")
        op_ok = sem("op_ok")
        res2_ok = sem("res2_ok")
        stats2_ok = sem("stats2_ok")
        rstd2_ok = sem("rstd2_ok")
        z2_ok = sem("z2_ok")
        xres2_ok = sem("xres2_ok")
        local_ok = sem("local_ok")
        uplocal_ok = sem("uplocal_ok")
        uplocal_sb = sem("uplocal_sb")
        upc_ok = sem("upc_ok")
        upt_ok = sem("upt_ok")
        upm_ok = sem("upm_ok")
        upb_sb = sem("upb_sb")
        downc_ok = sem("downc_ok")
        downm_ok = sem("downm_ok")
        downm_sb = sem("downm_sb")
        t2_ok = sem("t2_ok")
        zt2_ok = sem("zt2_ok")
        h_ok = sem("h_ok")
        gelu_ok = sem("gelu_ok")
        f_ok = sem("f_ok")
        res3_ok = sem("res3_ok")
        stats3_ok = sem("stats3_ok")
        rstd3_ok = sem("rstd3_ok")
        z3_ok = sem("z3_ok")
        out_done = sem("out_done")

        def tok(g):
            return slice(g * GT, (g + 1) * GT)

        def grp(g):
            return slice(g * GB, (g + 1) * GB)

        def head_tok(s, b, h):
            g, t = divmod(b, GB)
            return stack[s][0:SK, g % 2, h, t * T:(t + 1) * T]

        def quads(ap):
            return ap.rearrange("p (h t) -> p h t", h=HQ)

        block = ctx.enter_context(nc.Block())

        @block.sync
        def _(sp):
            def load(dst, src, s):
                sp.dma_start(dst, src).then_inc(s, 16)

            x_tok = x.rearrange("b t c -> t b c")
            load(x_sb[:, grp(0), :], x_tok[:, grp(0), :], x_in[0])
            load(col[:], columns, col_in)
            load(w_sb[:], weights, w_in)
            load(ctx_sb[:, 0, :], ctx_t[:, tok(0)], ctx_in[0])
            load(x_sb[:, grp(1), :], x_tok[:, grp(1), :], x_in[1])
            load(mask_sb[:], mask, mask_in)
            load(mask_t_sb[:], mask_t, mask_in)
            load(ctx_sb[:, 1, :], ctx_t[:, tok(1)], ctx_in[1])
            for i in range(3):
                load(row[:, i, :], rows[i:i + 1, :].broadcast_to([P, C]), row_in)
            for g in range(2, G):
                load(x_sb[:, grp(g), :], x_tok[:, grp(g), :], x_in[g])
            load(wexp_sb[:], w_exp_t, ffn_in)
            load(wcon_sb[:], w_con, ffn_in)
            load(local_w[:, 0, 0:n_local], up_local, ffn_in)
            load(local_w[:, 1, 0:n_local], down_local, ffn_in)
            load(cross_w[:, 0, :], up_cross, ffn_in)
            load(cross_w[:, 1, :], down_cross, ffn_in)

            def load_ctx(g):
                sp.wait_ge(kc_ok, g - 1)
                sp.wait_ge(vc_ok, g - 1)
                load(ctx_sb[:, g % 2, :], ctx_t[:, tok(g)], ctx_in[g])

            def spill_parts(s, g):
                sp.wait_ge([q_third, k_third][s], g + 1)
                sp.dma_start(spill[s][g].rearrange("n p t -> p n t"), part[s][:, g % 2, :, :]).then_inc(spilled[s][g], 16)

            def stack_rows(s, g):
                if g >= 2:
                    sp.wait_ge(s2_ok, NQ * GB * (g - 1))
                    if s == 0:
                        sp.dma_start(stack[0][SHIFT_ROW:SHIFT_ROW + NS, g % 2, :, :],
                                     stack[0][SK - NS:SK, g % 2, :, :]).then_inc(stack_zero[g % 2], 16)
                sp.wait_ge(spilled[s][g], 16)
                sp.wait_ge(stack_filled[s], min(g, 1) + 1)
                for n, pair in enumerate(PAIRS):
                    sp.dma_start(stack[s][n * D:(n + 1) * D, g % 2, :, :],
                                 spill[s][g, pair[s]].rearrange("(h d) t -> d h t", d=D))\
                      .then_inc(stack_in[s][g % 2], 16)

            def shift_rows(b):
                g, t = divmod(b, GB)
                sp.wait_ge(shiftt_sb, b + 1)
                for n in range(NS):
                    sp.dma_start(stack[0][SHIFT_ROW + n:SHIFT_ROW + n + 1, g % 2, :, t * T:(t + 1) * T],
                                 shift_t[n * H:(n + 1) * H, b % 2, :]).then_inc(shift_in[b % 2], 16)

            for g in range(G):
                spill_parts(1, g)
                if g + 2 < G:
                    load_ctx(g + 2)
            stack_rows(1, 0)
            for g in range(G):
                spill_parts(0, g)
                if g < 2:
                    stack_rows(0, g)
                if g == 0:
                    stack_rows(1, 1)
            for b in range(B):
                shift_rows(b)
                if b % GB == 2 and b >= GB and b // GB + 1 < G:
                    stack_rows(1, b // GB + 1)
                    stack_rows(0, b // GB + 1)
            out_tok = out.rearrange("b t c -> t b c")
            for g in range(G):
                sp.wait_ge(z3_ok, g + 1)
                sp.dma_start(out_tok[:, grp(g), :], z[:, grp(g), :]).then_inc(out_done, 16)
            sp.wait_ge(out_done, 16 * G)

        @block.gpsimd
        def _(pool):
            chain = [0]

            def link(ins):
                chain[0] += 1
                ins.then_inc(pool_own, 1)
                pool.wait_ge(pool_own, chain[0])

            nc.gpsimd.memset(ident[:], 0.0).then_inc(ident_0, 1)
            nc.gpsimd.memset(ident_bf[:], 0.0).then_inc(ident_0, 1)
            pool.wait_ge(ident_0, 2)
            for m in (ident, ident_bf):
                nc.gpsimd.affine_select(out=m[:], in_=m[:], compare_op=ALU.not_equal, fill=1.0, base=0,
                                        pattern=[[-1, P]], channel_multiplier=1).then_inc(ident_ok, 1)
            nc.gpsimd.memset(xn[:, :, :, 0:1], 0.0).then_inc(const_ok, 1)
            nc.gpsimd.memset(neg_half[:], -0.5).then_inc(const_ok, 1)
            nc.gpsimd.memset(one_cell[:], 1.0).then_inc(const_ok, 1)
            pool.wait_ge(const_ok, 3)

            def rstd_of(k, bs, last):
                n = bs.stop - bs.start
                r, m = rstd[:, k, bs], nmr[:, k, bs]
                link(nc.gpsimd.tensor_scalar(r, mv[:, bs, 1], EPS, None, ALU.add))
                link(nc.gpsimd.tensor_tensor(r, r, neg_half[:, 0:n], ALU.pow))
                link(nc.gpsimd.tensor_tensor(m, mv[:, bs, 0], r, ALU.mult))
                nc.gpsimd.tensor_scalar(m, m, -1.0, 0.0, ALU.mult, ALU.add).then_inc(last, 1)

            def add_row(g, r, done):
                nc.gpsimd.tensor_tensor(xres[:, grp(g), :], z[:, grp(g), :],
                                        r.to_broadcast([P, GB, C]), ALU.add).then_inc(done, 1)

            def stack_fill(s, half):
                two_ones = 1.0 + 0x3F80 * 2.0 ** -23
                nc.gpsimd.memset(stack[s][0:SK, half, :, :].rearrange("p h t -> p (h t)").bitcast(FP32),
                                 two_ones if s == 1 else 0.0).then_inc(stack_filled[s], 1)

            pool.wait_ge(col_in, 16)
            for s in range(G + 2):
                if s < G:
                    pool.wait_ge(stats_ok, s + 1)
                    rstd_of(0, grp(s), rstd_ok)
                if 0 <= s - 2 < G:
                    pool.wait_ge(stats1_ok, s - 1)
                    rstd_of(1, grp(s - 2), rstd1_ok)
                if s < 4:
                    stack_fill((1, 0, 1, 0)[s], s // 2)
                if 0 <= s - 2 < G:
                    pool.wait_ge(z1_ok, GB * (s - 1))
                    if s == 2:
                        pool.wait_ge(row_in, 48)
                    add_row(s - 2, row[:, 0:1, :], xres1_ok)

            pool.wait_ge(ffn_in, 96)
            at = 0
            for k in range(LOCAL):
                n = 2 ** k
                w = local_w[:, 0, at:at + 2 * n * FB].rearrange("p (f o j) -> p f o j", f=FB, o=2)
                dst = local_m[0][k % 2][:, 0:2 * n * FB].rearrange("p (f o j) -> p f o j", f=FB, o=2)
                src = local_m[0][(k + 1) % 2][:, 0:n * FB].rearrange("p (f j) -> p f j", f=FB)
                for o in range(2):
                    if k == 0:
                        ins = nc.gpsimd.tensor_copy(dst[:, :, o, :], w[:, :, o, :])
                    else:
                        ins = nc.gpsimd.tensor_tensor(dst[:, :, o, :], w[:, :, o, :], src, ALU.mult)
                    if k == LOCAL - 1:
                        ins.then_inc(local_ok, 1)
                    elif o == 1:
                        link(ins)
                    else:
                        link(ins)
                at += 2 * n * FB
            at = 0
            for k in range(LOCAL - 1, -1, -1):
                n = 2 ** (LOCAL - 1 - k)
                w = local_w[:, 1, at:at + 2 * n * FB].rearrange("p (f i) -> p f i", i=2)
                dst = local_m[1][k % 2][:, 0:2 * n * FB].rearrange("p (f i) -> p f i", i=2)
                src = local_m[1][(k + 1) % 2][:, 0:n * FB]
                for i in range(2):
                    if k == LOCAL - 1:
                        ins = nc.gpsimd.tensor_copy(dst[:, :, i], w[:, :, i])
                    else:
                        ins = nc.gpsimd.tensor_tensor(dst[:, :, i], w[:, :, i], src, ALU.mult)
                    if k == 0:
                        ins.then_inc(local_ok, 1)
                    else:
                        link(ins)
                at += 2 * n * FB

            def cross(side, src, stage, dst, last):
                s = 2 ** stage
                n = src.shape[-1]
                other = hidden[:].rearrange("p f t -> p (f t)")[:, 0:FB * n].rearrange("p (f c) -> p f c", f=FB)
                for b in range(FB):
                    bit = (b >> stage) & 1
                    lo, hi = b & ~s, b | s
                    pair = (b >> 1) if stage == 0 else (b & 1)
                    c0 = 8 * stage + 4 * pair + (2 * bit if side == 0 else bit)
                    c1 = c0 + (1 if side == 0 else 2)
                    nc.gpsimd.tensor_scalar(dst[:, b, :], src[:, lo, :], cross_w[:, side, c0:c0 + 1], 0.0,
                                            ALU.mult, ALU.add).then_inc(pool_own, 1)
                    nc.gpsimd.tensor_scalar(other[:, b, :], src[:, hi, :], cross_w[:, side, c1:c1 + 1], 0.0,
                                            ALU.mult, ALU.add).then_inc(pool_own, 1)
                    chain[0] += 2
                pool.wait_ge(pool_own, chain[0])
                ins = nc.gpsimd.tensor_tensor(dst, dst, other, ALU.add)
                if last is not None:
                    ins.then_inc(last, 1)
                    pool.wait_ge(last, 1)
                else:
                    link(ins)

            pool.wait_ge(local_ok, 4)
            cross(1, wcon_sb, 1, down_cross_m[:, 0], None)
            cross(1, down_cross_m[:, 0], 0, down_cross_m[:, 1], downc_ok)
            pool.wait_ge(uplocal_sb, 2)
            cross(0, up_rows, 0, up_cross_m[:, 0], None)
            cross(0, up_cross_m[:, 0], 1, up_cross_m[:, 1], upc_ok)
            link(nc.gpsimd.tensor_tensor(row_ffn[:], row[:, 1, :], row[:, 2, :], ALU.add))
            for b in range(B):
                pool.wait_ge(stats2_ok, b + 1)
                rstd_of(2, slice(b, b + 1), rstd2_ok)
                if b % GB == GB - 1:
                    g = b // GB
                    pool.wait_ge(z2_ok, b + 1)
                    add_row(g, row_ffn[:, None, :], xres2_ok)
            for g in range(G):
                pool.wait_ge(stats3_ok, g + 1)
                rstd_of(3, grp(g), rstd3_ok)

        @block.vector
        def _(dve):
            chain = [0]

            def link(ins):
                chain[0] += 1
                ins.then_inc(dve_own, 1)
                dve.wait_ge(dve_own, chain[0])

            def norm_stats(src, bs, done):
                for b in range(bs.start, bs.stop):
                    ins = nc.vector.bn_stats(stats[:, b, :], src[:, b, :])
                    ins.then_inc(dve_own, 1)
                    chain[0] += 1
                dve.wait_ge(dve_own, chain[0])
                for b in range(bs.start, bs.stop):
                    ins = nc.vector.bn_aggr(mv[:, b, :], stats[:, b, :])
                    if b < bs.stop - 1:
                        ins.then_inc(dve_own, 1)
                        chain[0] += 1
                dve.wait_ge(dve_own, chain[0])
                ins.then_inc(done, 1)

            nc.vector.memset(v_sb[:, :, :, D:VW], 1.0).then_inc(dve_const, 1)
            nc.vector.memset(decay_row[:], 1.0).then_inc(dve_const, 1)
            dve.wait_ge(dve_const, 2)

            dve.wait_ge(col_in, 16)
            dve.wait_ge(w_in, 16)
            link(nc.vector.tensor_scalar(one_less[:], col[:, C_MIXK:C_MIXK + 3], -1.0, 1.0, ALU.mult, ALU.add))
            for n in range(3):
                link(nc.vector.tensor_scalar(w_cur[:, n, :], w_sb[:, n, :], col[:, C_MIXK + n:C_MIXK + n + 1], None,
                                             ALU.mult))
                ins = nc.vector.tensor_scalar(w_last[:, n, :], w_sb[:, n, :], one_less[:, n:n + 1], None, ALU.mult)
                if n < 2:
                    link(ins)
            ins.then_inc(mixw_ok, 1)

            def wkv(g):
                e = g % 2
                if g == 0:
                    dve.wait_ge(decay_ok, 1)
                    link(nc.vector.tensor_scalar(decay_row[:], decay_row[:], decay[:, 0:1], None, ALU.mult))
                    link(nc.vector.memset(decay_row[:, :, 0:1], 0.0))
                dr = decay_row[:].rearrange("p b t -> p (b t)")
                dve.wait_ge(ek_ok, g + 1)
                dve.wait_ge(proj_ok, 3 * g + 2)
                nc.vector.tensor_tensor(ekv, ek[:, e, :], bank[2][:], ALU.mult).then_inc(ekv_ok, 1)
                link(nc.vector.tensor_tensor_scan(den, dr, ek[:, e, :], 0.0, ALU.mult, ALU.add))
                dve.wait_ge(ekv_ok, g + 1)
                link(nc.vector.tensor_tensor_scan(num, dr, ekv, 0.0, ALU.mult, ALU.add))
                dve.wait_ge(er_ok, g + 1)
                link(nc.vector.tensor_scalar(er[:, e, :], er[:, e, :], 1.0, None, ALU.add))
                link(nc.vector.scalar_tensor_tensor(den, den, DEN_EPS, er[:, e, :], ALU.add, ALU.mult))
                link(nc.vector.reciprocal(den, den))
                if g >= 2:
                    dve.wait_ge(y_ok, g - 1)
                nc.vector.tensor_tensor(gated[:, e, :], num, den, ALU.mult).then_inc(gated_ok, 1)
                dve.wait_ge(gated_ok, g + 1)

            def split(s, g, psum, scale, first, rest_s, second, third):
                p, r = part[s][:, g % 2], rest[:, s, :]
                dve.wait_ge(first, g + 1)
                nc.vector.scalar_tensor_tensor(r, psum, scale, p[:, 0, :], ALU.mult,
                                               ALU.subtract).then_inc(rest_s, 1)
                dve.wait_ge(rest_s, g + 1)
                nc.vector.tensor_copy(p[:, 1, :], r).then_inc(second, 1)
                dve.wait_ge(second, g + 1)
                nc.vector.tensor_tensor(p[:, 2, :], r, p[:, 1, :], ALU.subtract).then_inc(third, 1)
                dve.wait_ge(third, g + 1)

            def residual1(g):
                dve.wait_ge(y_ok, g + 1)
                nc.vector.tensor_tensor(x_sb[:, grp(g), :], x_sb[:, grp(g), :],
                                        bank[4][:].rearrange("p (b c) -> p b c", b=GB), ALU.add).then_inc(res1_ok, 1)
                dve.wait_ge(res1_ok, g + 1)
                norm_stats(x_sb, grp(g), stats1_ok)

            for s in range(G + 3):
                if s < G:
                    dve.wait_ge(x_in[s], 16)
                    norm_stats(x_sb, grp(s), stats_ok)
                if 0 <= s - 1 < G:
                    wkv(s - 1)
                if s < G:
                    dve.wait_ge(kc_ok, s + 1)
                    split(1, s, bank[7][:], 1.0, k_first, k_rest, k_second, k_third)
                if s == 0:
                    dve.wait_ge(mask_in, 32)
                    for m, b in ((mask_sb, bias_q), (mask_t_sb, bias_k)):
                        link(nc.vector.tensor_scalar(m[:], m[:], -1.0, 1.0, ALU.mult, ALU.add))
                        link(nc.vector.tensor_scalar(b[:], m[:], MASKED, None, ALU.mult))
                    link(nc.vector.tensor_reduce(bias_top[:], bias_q[:], AX.X, ALU.max))
                    nc.vector.tensor_scalar(bias_rel[:], bias_q[:], bias_top[:, 0:1], None,
                                            ALU.subtract).then_inc(bias_ok, 1)
                if 0 <= s - 2 < G:
                    residual1(s - 2)
                if 0 <= s - 3 < G:
                    g = s - 3
                    dve.wait_ge(q_ok, g + 1)
                    split(0, g, bank[6][:], QK_SCALE, q_first, q_rest, q_second, q_third)

            def quad_max(b, q):
                dve.wait_ge(s1_ok, NQ * b + q + 1)
                if q == 0 and b >= 2:
                    dve.wait_ge(shift_ok, b - 1)
                nc.vector.tensor_reduce(top[:, b % 2, q * HQ:(q + 1) * HQ], quads(bank[q % 2][:]), AX.X, ALU.max,
                                        negate=True).then_inc(max_ok, 1)

            def shift_parts(b):
                t = top[:, b % 2, :]
                dve.wait_ge(max_ok, NQ * (b + 1))
                if b >= 1:
                    dve.wait_ge(shiftt_ok, b)
                link(nc.vector.tensor_scalar(t, t, bias_top[:, 0:1], None, ALU.subtract))
                link(nc.vector.tensor_copy(shift[:, 0, :], t))
                link(nc.vector.tensor_tensor(top_rest[:], t, shift[:, 0, :], ALU.subtract))
                link(nc.vector.tensor_copy(shift[:, 1, :], top_rest[:]))
                nc.vector.tensor_tensor(shift[:, 2, :], top_rest[:], shift[:, 1, :], ALU.subtract).then_inc(shift_ok, 1)
                dve.wait_ge(shift_ok, b + 1)

            def add_bias(b, q):
                dve.wait_ge(s2_ok, NQ * b + q + 1)
                if q == 0 and b >= 2:
                    dve.wait_ge(av_ok, b - 1)
                nc.vector.tensor_tensor(probs[:, b % 2, q * HQ:(q + 1) * HQ, :], quads(bank[2 + q % 2][:]),
                                        bias_k[:, None, :].to_broadcast([P, HQ, T]), ALU.add).then_inc(added_ok, 1)

            def normalise(b):
                dve.wait_ge(ox_ok, b + 1)
                o = bank[6][:].rearrange("p (h r) -> p h r", r=STRIP)
                nc.vector.reciprocal(rden.rearrange("p (h o) -> p h o", o=1), o[:, :, D:D + 1]).then_inc(rden_ok, 1)
                dve.wait_ge(rden_ok, b + 1)
                if b >= 1:
                    dve.wait_ge(nt_ok, b)
                nc.vector.tensor_tensor(o_norm[:], o[:, :, 0:D],
                                        rden.rearrange("p (h o) -> p h o", o=1).to_broadcast([P, H, D]),
                                        ALU.mult).then_inc(norm_ok, 1)

            def residual2(b):
                dve.wait_ge(op_ok, b + 1)
                if b == 0:
                    dve.wait_ge(xres1_ok, G)
                nc.vector.tensor_tensor(x_sb[:, b, :], xres[:, b, :], bank[5][:, 256:256 + C],
                                        ALU.add).then_inc(res2_ok, 1)
                dve.wait_ge(res2_ok, b + 1)
                norm_stats(x_sb, slice(b, b + 1), stats2_ok)

            for s in range(B + 6):
                for q in range(NQ):
                    if s < B:
                        quad_max(s, q)
                    if 0 <= s - 2 < B:
                        add_bias(s - 2, q)
                    if q == 0 and 0 <= s - 4 < B:
                        normalise(s - 4)
                    if q == 2 and 0 <= s - 5 < B:
                        residual2(s - 5)
                if s < B:
                    shift_parts(s)

            dve.wait_ge(downm_ok, 1)
            nc.vector.tensor_copy(down_m[:].rearrange("p f c -> p (f c)"), bank[1][:]).then_inc(downm_sb, 1)
            dve.wait_ge(upc_ok, 1)
            nc.vector.tensor_tensor(up_b[:], up_cross_m[:, 1, :, C], col[:, C_UPB:C_UPB + FB], ALU.add).then_inc(upb_sb, 1)

            def ffn_input(g):
                dve.wait_ge(t2_ok, g + 1)
                if g >= 2:
                    dve.wait_ge(h_ok, FB * (g - 1))
                nc.vector.tensor_copy(zt[:, g % 2, :], bank[4 + g % 2][:]).then_inc(zt2_ok, 1)

            def residual3(g):
                dve.wait_ge(f_ok, g + 1)
                dve.wait_ge(xres2_ok, g + 1)
                nc.vector.tensor_tensor(x_sb[:, grp(g), :], xres[:, grp(g), :],
                                        bank[6 + g % 2][:].rearrange("p (b c) -> p b c", b=GB),
                                        ALU.add).then_inc(res3_ok, 1)
                dve.wait_ge(res3_ok, g + 1)
                norm_stats(x_sb, grp(g), stats3_ok)

            def output_rows(g):
                dve.wait_ge(rstd3_ok, g + 1)
                for b in range(g * GB, (g + 1) * GB):
                    ins = nc.vector.tensor_scalar(z[:, b, :], x_sb[:, b, :], rstd[:, 3, b:b + 1], nmr[:, 3, b:b + 1],
                                                  ALU.mult, ALU.add)
                    if b < (g + 1) * GB - 1:
                        link(ins)
                ins.then_inc(z3_ok, 1)

            ffn_input(0)
            for g in range(G + 1):
                if g + 1 < G:
                    ffn_input(g + 1)
                if g < G:
                    residual3(g)
                if g >= 1:
                    output_rows(g - 1)

        @block.scalar
        def _(act):
            act.wait_ge(col_in, 16)
            nc.scalar.activation(decay[:], col[:, C_DECAY:C_DECAY + 1], ACT.Exp).then_inc(decay_ok, 1)

            def apply_norm(k, bs, ready, n, done):
                act.wait_ge(ready, n)
                for b in range(bs.start, bs.stop):
                    nc.scalar.activation(z[:, b, :], x_sb[:, b, :], ACT.Identity, bias=nmr[:, k, b:b + 1],
                                         scale=rstd[:, k, b:b + 1]).then_inc(done, 1)

            for s in range(G + 3):
                if s < G:
                    apply_norm(0, grp(s), rstd_ok, s + 1, z0_ok)
                    act.wait_ge(t0_ok, s + 1)
                    if s == 0:
                        act.wait_ge(const_ok, 3)
                    if s >= 2:
                        act.wait_ge(proj_ok, 3 * (s - 1))
                    nc.scalar.activation(xn[:, s % 2, :, 1:T + 1], bank[0][:].rearrange("p (b t) -> p b t", b=GB),
                                         ACT.Identity, bias=col[:, C_B:C_B + 1],
                                         scale=col[:, C_G:C_G + 1]).then_inc(xn_ok, 1)
                    act.wait_ge(kc_ok, s + 1)
                    if s >= 2:
                        act.wait_ge(spilled[1][s - 2], 16)
                    nc.scalar.activation(part[1][:, s % 2, 0, :], bank[7][:], ACT.Copy).then_inc(k_first, 1)
                    act.wait_ge(vc_ok, s + 1)
                    if s == 0:
                        act.wait_ge(dve_const, 2)
                    nc.scalar.activation(v_sb[:, grp(s), :, 0:D],
                                         bank[5][:].rearrange("p (b h d) -> p b h d", b=GB, h=H),
                                         ACT.Copy).then_inc(v_ok, 1)
                if 0 <= s - 2 < G:
                    apply_norm(1, grp(s - 2), rstd1_ok, s - 1, z1_ok)
                if s < G:
                    act.wait_ge(proj_ok, 3 * s + 1)
                    if s >= 2:
                        act.wait_ge(gated_ok, s - 1)
                    nc.scalar.activation(ek[:, s % 2, :], bank[1][:], ACT.Exp).then_inc(ek_ok, 1)
                    act.wait_ge(proj_ok, 3 * s + 3)
                    nc.scalar.activation(er[:, s % 2, :], bank[3][:], ACT.Exp, scale=-1.0).then_inc(er_ok, 1)
                if 0 <= s - 2 < G:
                    g = s - 2
                    act.wait_ge(t1_ok, g + 1)
                    nc.scalar.activation(zt[:, g % 2, :], bank[5][:], ACT.Copy).then_inc(zt1_ok, 1)
                    act.wait_ge(q_ok, g + 1)
                    if g >= 2:
                        act.wait_ge(spilled[0][g - 2], 16)
                    nc.scalar.activation(part[0][:, g % 2, 0, :], bank[6][:], ACT.Copy,
                                         scale=QK_SCALE).then_inc(q_first, 1)

            def exps(b, q):
                act.wait_ge(added_ok, NQ * b + q + 1)
                p = probs[:, b % 2, q * HQ:(q + 1) * HQ, :]
                nc.scalar.activation(p, p, ACT.Exp).then_inc(exp_ok, 1)

            def shift_copy(b):
                act.wait_ge(shiftt_ok, b + 1)
                if b >= 2:
                    act.wait_ge(shift_in[b % 2], 48 * (b // 2))
                nc.scalar.activation(shift_t[:, b % 2, :], bank[7][0:NS * H, 0:T // 2].bitcast(BF16),
                                     ACT.Copy).then_inc(shiftt_sb, 1)

            for s in range(B + 6):
                if s == 3:
                    act.wait_ge(uplocal_ok, 1)
                    nc.scalar.activation(up_rows[:, :, 0:C], bank[7][:].rearrange("p (f c) -> p f c", f=FB),
                                         ACT.Copy).then_inc(uplocal_sb, 1)
                    nc.scalar.activation(up_rows[:, :, C], bank[6][:, 0:FB], ACT.Copy).then_inc(uplocal_sb, 1)
                for q in range(NQ):
                    if q == 0 and 0 <= s - 4 < B:
                        act.wait_ge(av_ok, s - 3)
                        if s - 4 >= 1:
                            act.wait_ge(ox_ok, s - 4)
                        nc.scalar.activation(o_t[:].rearrange("p g t -> p (g t)"), bank[4][:],
                                             ACT.Copy).then_inc(ot_ok, 1)
                    if q == 1 and 0 <= s - 1 < B:
                        shift_copy(s - 1)
                    if 0 <= s - 2 < B:
                        exps(s - 2, q)
                    if q == 2 and 0 <= s - 4 < B:
                        act.wait_ge(nt_ok, s - 3)
                        if s - 4 >= 1:
                            act.wait_ge(op_ok, s - 4)
                        nc.scalar.activation(o_norm_t[:], bank[7][:, 0:T], ACT.Copy).then_inc(ntsb_ok, 1)
                if 0 <= s - 5 < B:
                    b = s - 5
                    apply_norm(2, slice(b, b + 1), rstd2_ok, b + 1, z2_ok)

            act.wait_ge(upt_ok, 1)
            nc.scalar.activation(up_m[:].rearrange("p f c -> p (f c)"), bank[0][:], ACT.Copy).then_inc(upm_ok, 1)
            act.wait_ge(upb_sb, 1)
            for g in range(G):
                for f in range(FB):
                    act.wait_ge(h_ok, FB * g + f + 1)
                    if g >= 1 and f == 0:
                        act.wait_ge(f_ok, g)
                    nc.scalar.activation(hidden[:, f, :], bank[f % 2][:], ACT.Gelu,
                                         bias=up_b[:, f:f + 1]).then_inc(gelu_ok, 1)

        @block.tensor
        def _(pe):
            def mm(out_, lhs, rhs, start=True, stop=True, **kw):
                return nc.tensor.matmul(out_, lhs, rhs, start=start, stop=stop, **kw)

            def transposes(dst, g):
                for t in range(GB):
                    ins = nc.tensor.transpose(dst[:, t * T:(t + 1) * T], z[:, g * GB + t, :], ident[:])
                return ins

            def context(g):
                pe.wait_ge(ctx_in[g], 16)
                if g >= 1:
                    pe.wait_ge(k_rest, g)
                mm(bank[7][:], w_sb[:, X_K, :], ctx_sb[:, g % 2, :]).then_inc(kc_ok, 1)
                if g >= 1:
                    pe.wait_ge(v_ok, g)
                if g >= 3:
                    pe.wait_ge(zt1_ok, g - 2)
                for t in range(GB):
                    ins = mm(bank[5][:, t * C:(t + 1) * C], ctx_sb[:, g % 2, t * T:(t + 1) * T], w_sb[:, X_V, :])
                ins.then_inc(vc_ok, 1)

            def project_in(g):
                pe.wait_ge(z0_ok, GB * (g + 1))
                if g >= 1:
                    pe.wait_ge(xn_ok, g)
                transposes(bank[0], g).then_inc(t0_ok, 1)
                context(g)
                pe.wait_ge(xn_ok, g + 1)
                pe.wait_ge(mixw_ok, 1)
                for n, (free, w) in enumerate(((ek_ok, W_K), (ekv_ok, W_V), (er_ok, W_R))):
                    if g >= 1:
                        pe.wait_ge(free, g)
                    dst = bank[1 + n][:].rearrange("p (b t) -> p b t", b=GB)
                    mm(dst, w_cur[:, w, :], xn[:, g % 2, :, 1:T + 1], stop=False)
                    mm(dst, w_last[:, w, :], xn[:, g % 2, :, 0:T], start=False).then_inc(proj_ok, 1)

            def project_out(g):
                pe.wait_ge(gated_ok, g + 1)
                if g >= 1:
                    pe.wait_ge(res1_ok, g)
                for t in range(GB):
                    ins = mm(bank[4][:, t * C:(t + 1) * C], gated[:, g % 2, t * T:(t + 1) * T], w_sb[:, W_O, :])
                ins.then_inc(y_ok, 1)

            def project_q(g):
                pe.wait_ge(z1_ok, GB * (g + 1))
                pe.wait_ge(v_ok, min(g + 3, G))
                if g >= 1:
                    pe.wait_ge(zt1_ok, g)
                transposes(bank[5], g).then_inc(t1_ok, 1)
                pe.wait_ge(zt1_ok, g + 1)
                if g >= 1:
                    pe.wait_ge(q_rest, g)
                mm(bank[6][:], w_sb[:, X_Q, :], zt[:, g % 2, :]).then_inc(q_ok, 1)

            pe.wait_ge(ident_ok, 2)
            pe.wait_ge(w_in, 16)
            for s in range(G + 2):
                if s < G:
                    project_in(s)
                if 0 <= s - 1 < G:
                    project_out(s - 1)
                if 0 <= s - 2 < G:
                    project_q(s - 2)

            def scores(b, q):
                g = b // GB
                if b % GB == 0 and q == 0:
                    for s in range(2):
                        pe.wait_ge(stack_in[s][g % 2], 16 * len(PAIRS) * (g // 2 + 1))
                    if g >= 2:
                        pe.wait_ge(stack_zero[g % 2], 16 * (g // 2))
                if NQ * b + q >= 2:
                    pe.wait_ge(max_ok, NQ * b + q - 1)
                mm(quads(bank[q % 2][:]), ident_bf[:], bias_rel[:, None, :].to_broadcast([P, HQ, T]), stop=False,
                   skip_group_check=True)
                for j in range(HQ):
                    h = HQ * q + j
                    ins = mm(bank[q % 2][:, j * T:(j + 1) * T], head_tok(0, b, h), head_tok(1, b, h), start=False,
                             stop=(j == HQ - 1), skip_group_check=True)
                ins.then_inc(s1_ok, 1)

            def scores_t(b, q):
                if q == 0:
                    pe.wait_ge(shift_in[b % 2], 48 * (b // 2 + 1))
                if NQ * b + q >= 2:
                    pe.wait_ge(added_ok, NQ * b + q - 1)
                for j in range(HQ):
                    h = HQ * q + j
                    ins = mm(bank[2 + q % 2][:, j * T:(j + 1) * T], head_tok(1, b, h), head_tok(0, b, h))
                ins.then_inc(s2_ok, 1)

            def values(b, q):
                pe.wait_ge(exp_ok, NQ * b + q + 1)
                if q == 0 and b >= 1:
                    pe.wait_ge(ot_ok, b)
                for j in range(HQ):
                    h = HQ * q + j
                    ins = mm(bank[4][STRIP * j:STRIP * j + VW, q * T:(q + 1) * T], v_sb[:, b, h, :],
                             probs[:, b % 2, h, :])
                if q == NQ - 1:
                    ins.then_inc(av_ok, 1)

            up_l = local_m[0][(LOCAL - 1) % 2][:].rearrange("p (f j) -> p f j", f=FB)
            down_l = local_m[1][0][:].rearrange("p (f j) -> p f j", f=FB)
            pe.wait_ge(bias_ok, 1)
            pe.wait_ge(dve_const, 2)
            pe.wait_ge(er_ok, G)
            pe.wait_ge(ekv_ok, G)
            pe.wait_ge(res1_ok, G)
            pe.wait_ge(q_rest, G)
            pe.wait_ge(zt1_ok, G)
            pe.wait_ge(k_rest, G)
            for s in range(B + 6):
                for q in range(NQ):
                    if s < B:
                        scores(s, q)
                    if s == 3 and q == 0:
                        pe.wait_ge(uplocal_sb, 2)
                    if q == 0 and 0 <= s - 4 < B:
                        pe.wait_ge(ot_ok, s - 3)
                        if s - 4 >= 1:
                            pe.wait_ge(norm_ok, s - 4)
                        for n in range(NQ):
                            ins = nc.tensor.transpose(bank[6][:, n * T:(n + 1) * T], o_t[:, n, :], ident[:])
                        ins.then_inc(ox_ok, 1)
                    if 0 <= s - 2 < B:
                        scores_t(s - 2, q)
                    if q == 0 and 0 <= s - 1 < B:
                        pe.wait_ge(shift_ok, s)
                        if s - 5 >= 0:
                            pe.wait_ge(ntsb_ok, s - 4)
                        nc.tensor.transpose(bank[7][0:NS * H, 0:T // 2].bitcast(BF16),
                                            shift[:].rearrange("p n h -> p (n h)"), ident_bf[:]).then_inc(shiftt_ok, 1)
                    if 0 <= s - 3 < B:
                        values(s - 3, q)
                    if s == 2 and q == NQ - 1:
                        pe.wait_ge(local_ok, 4)
                        pe.wait_ge(shiftt_sb, 2)
                        for f in range(FB):
                            mm(bank[7][:, f * C:(f + 1) * C], up_l[:, f, :], wexp_sb[:, f, 0:C])
                            ins = mm(bank[6][:, f:f + 1], up_l[:, f, :], wexp_sb[:, f, C:C + 1])
                        ins.then_inc(uplocal_ok, 1)
                    if q == 2 and 0 <= s - 4 < B:
                        pe.wait_ge(norm_ok, s - 3)
                        pe.wait_ge(shiftt_sb, min(s, B))
                        nc.tensor.transpose(bank[7][:, 0:T], o_norm[:].rearrange("p h d -> p (h d)"),
                                            ident[:]).then_inc(nt_ok, 1)
                    if q == 3 and 0 <= s - 4 < B:
                        pe.wait_ge(ntsb_ok, s - 3)
                        if s - 4 >= 1:
                            pe.wait_ge(res2_ok, s - 4)
                        mm(bank[5][:, 256:256 + C], o_norm_t[:], w_sb[:, X_O, :]).then_inc(op_ok, 1)

            pe.wait_ge(max_ok, NQ * B)
            pe.wait_ge(downc_ok, 1)
            for f in range(FB):
                ins = mm(bank[1][:, f * C:(f + 1) * C], down_l[:, f, :], down_cross_m[:, 1, f, :])
            ins.then_inc(downm_ok, 1)
            pe.wait_ge(upc_ok, 1)
            for f in range(FB):
                ins = nc.tensor.transpose(bank[0][:, f * P:(f + 1) * P], up_cross_m[:, 1, f, 0:C], ident[:])
            ins.then_inc(upt_ok, 1)

            def ffn_turn(g):
                pe.wait_ge(z2_ok, GB * (g + 1))
                if g < 2:
                    pe.wait_ge((ot_ok, op_ok)[g], B)
                    pe.wait_ge(res2_ok, B)
                else:
                    pe.wait_ge(zt2_ok, g - 1)
                transposes(bank[4 + g % 2], g).then_inc(t2_ok, 1)

            def ffn_hidden(g):
                pe.wait_ge(zt2_ok, g + 1)
                for f in range(FB):
                    n = FB * g + f
                    if n < 2:
                        pe.wait_ge((upm_ok, downm_sb)[n], 1)
                        pe.wait_ge(upm_ok, 1)
                    else:
                        pe.wait_ge(gelu_ok, n - 1)
                    mm(bank[f % 2][:], up_m[:, f, :], zt[:, g % 2, :]).then_inc(h_ok, 1)

            def ffn_out(g):
                if g < 2:
                    pe.wait_ge((norm_ok, ntsb_ok)[g], B)
                else:
                    pe.wait_ge(res3_ok, g - 1)
                pe.wait_ge(gelu_ok, FB * (g + 1))
                for t in range(GB):
                    for f in range(FB):
                        ins = mm(bank[6 + g % 2][:, t * C:(t + 1) * C], hidden[:, f, t * T:(t + 1) * T],
                                 down_m[:, f, :], start=(f == 0), stop=(f == FB - 1))
                ins.then_inc(f_ok, 1)

            ffn_turn(0)
            for g in range(G):
                ffn_hidden(g)
                if g + 1 < G:
                    ffn_turn(g + 1)
                ffn_out(g)


def kernel(**inputs):
    import numpy as np
    import concourse.bacc as bacc
    from concourse.bass_utils import run_bass_kernel_spmd

    def f(name):
        return np.asarray(inputs[name])

    P, FB, LOCAL = 128, 4, 7
    x = f("x")
    attn = {n: f("L0_attn_" + n) for n in ("time_decay", "time_mix_k", "time_mix_v", "time_mix_r",
                                           "Wk", "Wv", "Wr", "Wo", "ln_g", "ln_b")}
    weights = np.stack([attn["Wk"].T, attn["Wv"].T, attn["Wr"].T, attn["Wo"].T,
                        f("L0_xattn_Wq"), f("L0_xattn_Wk"), f("L0_xattn_Wv"), f("L0_xattn_Wo")], axis=1)
    columns = np.concatenate(
        [attn[n].reshape(P, 1) for n in ("time_decay", "time_mix_k", "time_mix_v", "time_mix_r", "ln_g", "ln_b")]
        + [f("L0_ffn_up_bias").reshape(FB, P).T], axis=1)
    rows = np.stack([f("L0_xattn_bo"), f("L0_ffn_b_con"), f("L0_ffn_down_bias")])
    w_exp_t = np.concatenate([f("L0_ffn_W_exp").T.reshape(FB, P, P), f("L0_ffn_b_exp").reshape(FB, P, 1)],
                             axis=2).transpose(1, 0, 2)
    w_con = f("L0_ffn_W_con").reshape(FB, P, P).transpose(1, 0, 2)

    def up_local(w):
        p, blk = np.arange(P)[:, None, None, None], np.arange(FB)[None, :, None, None]
        parts = []
        for k in range(LOCAL):
            bit, low = np.arange(2)[None, None, :, None], np.arange(2 ** k)[None, None, None, :]
            pair = ((blk * P + p) >> (k + 1) << k) + low
            parts.append(w[k][pair, bit, (p >> k) & 1].reshape(P, -1))
        return np.concatenate(parts, axis=1)

    def down_local(w):
        p, blk = np.arange(P)[:, None, None, None], np.arange(FB)[None, :, None, None]
        parts = []
        for k in range(LOCAL - 1, -1, -1):
            n = 2 ** (LOCAL - 1 - k)
            high, bit = np.arange(n)[None, None, :, None], np.arange(2)[None, None, None, :]
            pair = ((blk * n + high) << k) + (p & (2 ** k - 1))
            parts.append(w[k][pair, (p >> k) & 1, bit].reshape(P, -1))
        return np.concatenate(parts, axis=1)

    def cross(w):
        return np.stack([w[k].reshape(2, P, 2, 2).transpose(1, 0, 2, 3) for k in (LOCAL, LOCAL + 1)],
                        axis=1).reshape(P, 16)

    up, down = f("L0_ffn_up_weights"), f("L0_ffn_down_weights")
    mask = f("mask_1x1xSxS2_fk0")[0, 0]
    arrays = {
        "x": x, "ctx_t": f("ctx_1024").transpose(2, 0, 1).reshape(P, -1), "mask": mask, "mask_t": mask.T,
        "weights": weights, "columns": columns, "rows": rows, "w_exp_t": w_exp_t, "w_con": w_con,
        "up_local": up_local(up), "down_local": down_local(down), "up_cross": cross(up), "down_cross": cross(down),
    }
    nc = bacc.Bacc("TRN2", target_bir_lowering=False, num_devices=1)
    given, args = {}, []
    for name, a in arrays.items():
        a = np.ascontiguousarray(a)
        given[f"in_{name}"] = a
        args.append(nc.dram_tensor(f"in_{name}", a.shape, mybir.dt.from_np(a.dtype), kind="ExternalInput").ap())
    args.append(nc.dram_tensor("out_y", x.shape, FP32, kind="ExternalOutput").ap())
    decoder_program(nc, *args)
    r = run_bass_kernel_spmd(nc, [given], core_ids=[0])
    return r.results[0]["out_y"]
```

```python
from contextlib import ExitStack

import concourse.bass as bass
from concourse import mybir

FP32 = mybir.dt.float32
BF16 = mybir.dt.bfloat16
ALU = mybir.AluOpType
ACT = mybir.ActivationFunctionType
AX = mybir.AxisListType


def decoder_program(nc, x, ctx_t, mask, mask_t, weights, columns, rows, w_exp_t, w_con,
                    up_local, down_local, up_cross, down_cross, out):
    P = 128
    B = x.shape[0]
    C = x.shape[2]
    T = x.shape[1]
    GB = 4
    G = B // GB
    GT = GB * T
    H = 16
    D = C // H
    HQ = 4
    NQ = H // HQ
    VW = D + 1
    STRIP = 32
    FB = w_exp_t.shape[1]
    LOCAL = 7
    EPS = 1e-5
    DEN_EPS = 1e-8
    MASKED = -1000000000.0
    QK_SCALE = float(D) ** -0.5
    PAIRS = [(0, 0), (0, 1), (0, 2), (1, 0), (1, 1), (2, 0)]
    RUNS = [[(n, p[0], 1) for n, p in enumerate(PAIRS)], [(0, 0, 3), (3, 0, 2), (5, 0, 1)]]
    SHIFT_ROW = len(PAIRS) * D
    NS = 3
    SK = 96
    C_DECAY, C_MIXK, C_MIXV, C_MIXR, C_G, C_B, C_UPB = range(7)
    W_K, W_V, W_R, W_O, X_Q, X_K, X_V, X_O = range(8)

    UP_AT = 3
    DOWN_AT = 8
    HIDDEN_AT = (11, 15)
    OUT_AT = (14, 18)

    PE_QUADS = (3,)

    ctx = ExitStack()
    with ctx:
        def sb(name, shape, dt=FP32):
            return ctx.enter_context(nc.sbuf_tensor(name, shape, dt))

        def sem(name):
            return ctx.enter_context(nc.semaphore(name))

        w_sb = sb("w_sb", [P, 8, C])
        col = sb("col", [P, columns.shape[1]])
        row = sb("row", [P, 3, C])
        row_ffn = sb("row_ffn", [P, C])
        ident = sb("ident", [P, P])
        ident_bf = sb("ident_bf", [P, P], BF16)
        one_col = sb("one_col", [P, 1])
        one_less = sb("one_less", [P, 3])
        neg_half = sb("neg_half", [P, GB])
        decay = sb("decay", [P, 1])
        decay_row = sb("decay_row", [P, GB, T])
        mask_sb = sb("mask_sb", [P, T])
        mask_t_sb = sb("mask_t_sb", [P, T])
        bias_q = sb("bias_q", [P, T])
        bias_top = sb("bias_top", [P, 1])
        bias_rel = sb("bias_rel", [P, T], BF16)
        bias_k = sb("bias_k", [P, T])
        bias_part = sb("bias_part", [P, 3, T], BF16)
        bias_rest = sb("bias_rest", [P, T])

        x_sb = sb("x_sb", [P, B, C])
        xres = sb("xres", [P, B, C])
        ctx_sb = sb("ctx_sb", [P, 2, GT])
        stats = sb("stats", [P, B, 6])
        mv = sb("mv", [P, B, 2])
        rstd = sb("rstd", [P, 4, B])
        nmr = sb("nmr", [P, 4, B])
        z = sb("z", [P, B, C])
        xn = sb("xn", [P, 2, GB, T + 1])
        hidden = sb("hidden", [P, FB, GT])
        w_cur = sb("w_cur", [P, 3, C])
        w_last = sb("w_last", [P, 3, C])
        ek = sb("ek", [P, 2, GT])
        er = sb("er", [P, 2, GT])
        early = sb("early", [P, 5, GT])
        ekv, den, num, gated = early[:, 0, :], early[:, 1, :], early[:, 2, :], early[:, 3:5, :]
        zt = sb("zt", [P, 2, GT])
        part = [sb(f"part_{s}", [P, 2, 3, GT], BF16) for s in "qk"]
        rest = sb("rest", [P, 2, GT])
        stack = [sb(f"stack_{s}", [P, 2, H, GT], BF16) for s in "qk"]
        v_sb = sb("v_sb", [P, B, H, VW])
        probs = sb("probs", [P, 2, H, T])
        top = sb("top", [P, 2, H])
        top_rest = sb("top_rest", [P, H])
        shift = sb("shift", [P, NS, H], BF16)
        shift_t = sb("shift_t", [NS * H, 2, T], BF16)
        o_t = sb("o_t", [P, NQ, T])
        rden = sb("rden", [P, H])
        o_norm = sb("o_norm", [P, H, D])
        o_norm_t = sb("o_norm_t", [P, T])
        wexp_sb = sb("wexp_sb", [P, FB, C + 1])
        wcon_sb = sb("wcon_sb", [P, FB, C])
        n_local = FB * (2 ** (LOCAL + 1) - 2)
        local_w = sb("local_w", [P, 2, 2 * FB * (C + 1)])
        local_m = [[sb(f"local_m{s}{i}", [P, FB * P >> i]) for i in range(2)] for s in range(2)]
        cross_w = sb("cross_w", [P, 2, 16])
        early_flat = early[:].rearrange("p n t -> p (n t)")
        up_rows = early_flat[:, 0:FB * (C + 1)].rearrange("p (f c) -> p f c", f=FB)
        up_cross_m = local_w[:, 0, :].rearrange("p (n f c) -> p n f c", n=2, f=FB)
        down_cross_m = local_w[:, 1, 0:2 * FB * C].rearrange("p (n f c) -> p n f c", n=2, f=FB)
        up_m = early_flat[:, 2 * GT:3 * GT].rearrange("p (f c) -> p f c", f=FB)
        down_m = early_flat[:, 3 * GT:4 * GT].rearrange("p (f c) -> p f c", f=FB)
        up_b = sb("up_b", [P, FB])

        spill = [nc.dram_tensor(f"spill_{s}", [G, 3, P, GT], BF16, kind="Internal").ap() for s in "qk"]

        bank = [ctx.enter_context(nc.psum_tensor(f"bank{i}", [P, 512], FP32)) for i in range(8)]

        w_in, col_in, row_in, mask_in, x_in, ctx_in, ffn_in = [sem(n) for n in (
            "w_in", "col_in", "row_in", "mask_in", "x_in", "ctx_in", "ffn_in")]
        x_in = [sem(f"x_in{g}") for g in range(G)]
        ctx_in = [sem(f"ctx_in{g}") for g in range(G)]
        ident_0 = sem("ident_0")
        ident_1 = sem("ident_1")
        ident_ok = sem("ident_ok")
        const_ok = sem("const_ok")
        dve_const = sem("dve_const")
        decay_ok = sem("decay_ok")
        bias_ok = sem("bias_ok")
        dve_own = sem("dve_own")
        pool_own = sem("pool_own")
        stats_ok = sem("stats_ok")
        rstd_ok = sem("rstd_ok")
        z0_ok = sem("z0_ok")
        t0_ok = sem("t0_ok")
        xn_ok = sem("xn_ok")
        mixw_ok = sem("mixw_ok")
        proj_ok = sem("proj_ok")
        ek_ok = sem("ek_ok")
        er_raw = sem("er_raw")
        er_ok = sem("er_ok")
        ekv_ok = sem("ekv_ok")
        num_ok = sem("num_ok")
        gated_ok = sem("gated_ok")
        y_ok = sem("y_ok")
        res1_ok = sem("res1_ok")
        stats1_ok = sem("stats1_ok")
        rstd1_ok = sem("rstd1_ok")
        z1_ok = sem("z1_ok")
        xres1_ok = sem("xres1_ok")
        t1_ok = sem("t1_ok")
        zt1_ok = sem("zt1_ok")
        q_ok = sem("q_ok")
        q_first = sem("q_first")
        q_rest = sem("q_rest")
        q_second = sem("q_second")
        q_third = sem("q_third")
        kc_ok = sem("kc_ok")
        k_first = sem("k_first")
        k_rest = sem("k_rest")
        k_second = sem("k_second")
        k_third = sem("k_third")
        vc_ok = sem("vc_ok")
        v_ok = sem("v_ok")
        stack_in = [[sem(f"stack_{s}_in{i}") for i in range(2)] for s in "qk"]
        spilled = [[sem(f"spilled_{s}{g}") for g in range(G)] for s in "qk"]
        stack_zero = [sem(f"stack_zero{i}") for i in range(2)]
        stack_filled = [sem(f"stack_{s}_filled") for s in "qk"]
        pad_in = [sem(f"pad_{s}_in") for s in "qk"]
        s1_ok = sem("s1_ok")
        max_ok = sem("max_ok")
        shift_ok = sem("shift_ok")
        shiftt_ok = sem("shiftt_ok")
        shiftt_sb = sem("shiftt_sb")
        shift_in = [sem(f"shift_in{i}") for i in range(2)]
        s2_ok = sem("s2_ok")
        added_ok = sem("added_ok")
        exp_ok = sem("exp_ok")
        av_ok = sem("av_ok")
        ot_ok = sem("ot_ok")
        ox_ok = sem("ox_ok")
        rden_ok = sem("rden_ok")
        norm_ok = sem("norm_ok")
        nt_ok = sem("nt_ok")
        ntsb_ok = sem("ntsb_ok")
        op_ok = sem("op_ok")
        res2_ok = sem("res2_ok")
        stats2_ok = sem("stats2_ok")
        rstd2_ok = sem("rstd2_ok")
        z2_ok = sem("z2_ok")
        xres2_ok = sem("xres2_ok")
        local_ok = sem("local_ok")
        uplocal_ok = sem("uplocal_ok")
        uplocal_sb = sem("uplocal_sb")
        upc_ok = sem("upc_ok")
        upt_ok = sem("upt_ok")
        upm_ok = sem("upm_ok")
        upb_sb = sem("upb_sb")
        downc_ok = sem("downc_ok")
        downm_ok = sem("downm_ok")
        downm_sb = sem("downm_sb")
        t2_ok = sem("t2_ok")
        zt2_ok = sem("zt2_ok")
        h_ok = sem("h_ok")
        h_sb = sem("h_sb")
        gelu_ok = sem("gelu_ok")
        f_ok = sem("f_ok")
        res3_ok = sem("res3_ok")
        stats3_ok = sem("stats3_ok")
        rstd3_ok = sem("rstd3_ok")
        z3_ok = sem("z3_ok")
        out_done = sem("out_done")

        def tok(g):
            return slice(g * GT, (g + 1) * GT)

        def grp(g):
            return slice(g * GB, (g + 1) * GB)

        def head_tok(s, b, h):
            g, t = divmod(b, GB)
            return stack[s][0:SK, g % 2, h, t * T:(t + 1) * T]

        def bias_on_pe(b, q):
            return q in PE_QUADS

        def added_before(b, q):
            return (NQ - len(PE_QUADS)) * b + sum(not bias_on_pe(b, i) for i in range(q))

        def quads(ap):
            return ap.rearrange("p (h t) -> p h t", h=HQ)

        block = ctx.enter_context(nc.Block())

        @block.sync
        def _(sp):
            def load(dst, src, s):
                sp.dma_start(dst, src).then_inc(s, 16)

            x_tok = x.rearrange("b t c -> t b c")
            load(x_sb[:, grp(0), :], x_tok[:, grp(0), :], x_in[0])
            load(col[:], columns, col_in)
            load(w_sb[:], weights, w_in)
            load(ctx_sb[:, 0, :], ctx_t[:, tok(0)], ctx_in[0])
            load(x_sb[:, grp(1), :], x_tok[:, grp(1), :], x_in[1])
            load(mask_sb[:], mask, mask_in)
            load(mask_t_sb[:], mask_t, mask_in)
            load(ctx_sb[:, 1, :], ctx_t[:, tok(1)], ctx_in[1])
            for i in range(3):
                load(row[:, i, :], rows[i:i + 1, :].broadcast_to([P, C]), row_in)
            for g in range(2, G):
                load(x_sb[:, grp(g), :], x_tok[:, grp(g), :], x_in[g])
            load(wexp_sb[:], w_exp_t, ffn_in)
            load(wcon_sb[:], w_con, ffn_in)
            load(local_w[:, 0, 0:n_local], up_local, ffn_in)
            load(local_w[:, 1, 0:n_local], down_local, ffn_in)
            load(cross_w[:, 0, :], up_cross, ffn_in)
            load(cross_w[:, 1, :], down_cross, ffn_in)

            def load_ctx(g):
                sp.wait_ge(kc_ok, g - 1)
                sp.wait_ge(vc_ok, g - 1)
                load(ctx_sb[:, g % 2, :], ctx_t[:, tok(g)], ctx_in[g])

            def spill_parts(s, g):
                sp.wait_ge([q_third, k_third][s], g + 1)
                sp.dma_start(spill[s][g].rearrange("n p t -> p n t"), part[s][:, g % 2, :, :]).then_inc(spilled[s][g], 16)

            def stack_rows(s, g):
                if g >= 2:
                    sp.wait_ge(s2_ok, NQ * GB * (g - 1))
                    if s == 0:
                        sp.dma_start(stack[0][SHIFT_ROW:SHIFT_ROW + NS, g % 2, :, :],
                                     stack[0][SK - NS:SK, g % 2, :, :]).then_inc(stack_zero[g % 2], 16)
                sp.wait_ge(spilled[s][g], 16)
                sp.wait_ge(stack_filled[s], 1)
                for n, first, count in RUNS[s]:
                    sp.dma_start(stack[s][n * D:(n + count) * D, g % 2, :, :],
                                 spill[s][g, first:first + (count if s == 1 else 1)]
                                 .rearrange("n (d h) t -> (n d) h t", d=D)).then_inc(stack_in[s][g % 2], 16)

            def shift_rows(b):
                g, t = divmod(b, GB)
                sp.wait_ge(shiftt_sb, b + 1)
                for n in range(NS):
                    sp.dma_start(stack[0][SHIFT_ROW + n:SHIFT_ROW + n + 1, g % 2, :, t * T:(t + 1) * T],
                                 shift_t[n * H:(n + 1) * H, b % 2, :]).then_inc(shift_in[b % 2], 16)

            def pad_rows(s):
                sp.wait_ge(stack_filled[s], 1)
                sp.dma_start(stack[s][SHIFT_ROW:SK, 1, :, :], stack[s][SHIFT_ROW:SK, 0, :, :]).then_inc(pad_in[s], 16)

            load_ctx(2)
            spill_parts(1, 0)
            load_ctx(3)
            pad_rows(1)
            stack_rows(1, 0)
            pad_rows(0)
            spill_parts(1, 1)
            stack_rows(1, 1)
            spill_parts(1, 2)
            spill_parts(0, 0)
            stack_rows(0, 0)
            spill_parts(1, 3)
            spill_parts(0, 1)
            shift_rows(0)
            stack_rows(0, 1)
            for b in range(1, B):
                if b + 1 < G:
                    spill_parts(0, b + 1)
                shift_rows(b)
                if b % GB == 1 and b >= GB and b // GB + 1 < G:
                    stack_rows(1, b // GB + 1)
                    stack_rows(0, b // GB + 1)
            out_tok = out.rearrange("b t c -> t b c")
            for g in range(G):
                sp.wait_ge(z3_ok, g + 1)
                sp.dma_start(out_tok[:, grp(g), :], z[:, grp(g), :]).then_inc(out_done, 16)
            sp.wait_ge(out_done, 16 * G)

        @block.gpsimd
        def _(pool):
            chain = [0]

            def link(ins):
                chain[0] += 1
                ins.then_inc(pool_own, 1)
                pool.wait_ge(pool_own, chain[0])

            nc.gpsimd.memset(ident[:], 0.0).then_inc(ident_0, 1)
            nc.gpsimd.memset(ident_bf[:], 0.0).then_inc(ident_0, 1)
            pool.wait_ge(ident_0, 2)
            for m in (ident, ident_bf):
                nc.gpsimd.affine_select(out=m[:], in_=m[:], compare_op=ALU.not_equal, fill=1.0, base=0,
                                        pattern=[[-1, P]], channel_multiplier=1).then_inc(ident_ok, 1)
            nc.gpsimd.memset(xn[:, :, :, 0:1], 0.0).then_inc(const_ok, 1)
            nc.gpsimd.memset(neg_half[:], -0.5).then_inc(const_ok, 1)
            nc.gpsimd.memset(one_col[:], 1.0).then_inc(const_ok, 1)
            pool.wait_ge(const_ok, 3)

            def rstd_of(k, bs, last):
                n = bs.stop - bs.start
                r, m = rstd[:, k, bs], nmr[:, k, bs]
                link(nc.gpsimd.tensor_scalar(r, mv[:, bs, 1], EPS, None, ALU.add))
                link(nc.gpsimd.tensor_tensor(r, r, neg_half[:, 0:n], ALU.pow))
                link(nc.gpsimd.tensor_tensor(m, mv[:, bs, 0], r, ALU.mult))
                nc.gpsimd.tensor_scalar(m, m, -1.0, 0.0, ALU.mult, ALU.add).then_inc(last, 1)

            def gate(g):
                pool.wait_ge(num_ok, g + 1)
                if g >= 2:
                    pool.wait_ge(y_ok, g - 1)
                nc.gpsimd.tensor_tensor(gated[:, g % 2, :], num, den, ALU.mult).then_inc(gated_ok, 1)

            def third_part(s, g, rest_s, second, third):
                pool.wait_ge(second, g + 1)
                nc.gpsimd.tensor_tensor(part[s][:, g % 2, 2, :], rest[:, s, :], part[s][:, g % 2, 1, :],
                                        ALU.subtract).then_inc(third, 1)

            def add_row(g, r, done):
                nc.gpsimd.tensor_tensor(xres[:, grp(g), :], z[:, grp(g), :],
                                        r.to_broadcast([P, GB, C]), ALU.add).then_inc(done, 1)

            def stack_fill(s, half):
                two_ones = 1.0 + 0x3F80 * 2.0 ** -23
                nc.gpsimd.memset(stack[s][0:SK, half, :, :].rearrange("p h t -> p (h t)").bitcast(FP32),
                                 two_ones if s == 1 else 0.0).then_inc(stack_filled[s], 1)

            def local_up():
                pool.wait_ge(ffn_in, 96)
                at = 0
                for k in range(LOCAL):
                    n = 2 ** k
                    w = local_w[:, 0, at:at + 2 * n * FB].rearrange("p (f o j) -> p f o j", f=FB, o=2)
                    dst = local_m[0][k % 2][:, 0:2 * n * FB].rearrange("p (f o j) -> p f o j", f=FB, o=2)
                    src = local_m[0][(k + 1) % 2][:, 0:n * FB].rearrange("p (f j) -> p f j", f=FB)
                    for o in range(2):
                        if k == 0:
                            ins = nc.gpsimd.tensor_copy(dst[:, :, o, :], w[:, :, o, :])
                        else:
                            ins = nc.gpsimd.tensor_tensor(dst[:, :, o, :], w[:, :, o, :], src, ALU.mult)
                        if k == LOCAL - 1:
                            ins.then_inc(local_ok, 1)
                        elif o == 1:
                            link(ins)
                        else:
                            link(ins)
                    at += 2 * n * FB

            def local_down():
                at = 0
                for k in range(LOCAL - 1, -1, -1):
                    n = 2 ** (LOCAL - 1 - k)
                    w = local_w[:, 1, at:at + 2 * n * FB].rearrange("p (f i) -> p f i", i=2)
                    dst = local_m[1][k % 2][:, 0:2 * n * FB].rearrange("p (f i) -> p f i", i=2)
                    src = local_m[1][(k + 1) % 2][:, 0:n * FB]
                    for i in range(2):
                        if k == LOCAL - 1:
                            ins = nc.gpsimd.tensor_copy(dst[:, :, i], w[:, :, i])
                        else:
                            ins = nc.gpsimd.tensor_tensor(dst[:, :, i], w[:, :, i], src, ALU.mult)
                        if k == 0:
                            ins.then_inc(local_ok, 1)
                        else:
                            link(ins)
                    at += 2 * n * FB


            for s in range(-1, G + 4):
                if 0 <= s + 1 < G:
                    pool.wait_ge(stats_ok, s + 2)
                    rstd_of(0, grp(s + 1), rstd_ok)
                if 0 <= s - 4 < G:
                    third_part(0, s - 4, q_rest, q_second, q_third)
                if 0 <= s - 1 < G:
                    third_part(1, s - 1, k_rest, k_second, k_third)
                    gate(s - 1)
                if 0 <= s - 2 < G:
                    pool.wait_ge(stats1_ok, s - 1)
                    rstd_of(1, grp(s - 2), rstd1_ok)
                if s == 0:
                    stack_fill(1, 0)
                    stack_fill(0, 0)
                    local_up()
                if 0 <= s - 3 < G:
                    pool.wait_ge(z1_ok, GB * (s - 2))
                    if s == 3:
                        pool.wait_ge(row_in, 48)
                    add_row(s - 3, row[:, 0:1, :], xres1_ok)
            local_down()

            def cross(side, src, stage, dst, last):
                s = 2 ** stage
                n = src.shape[-1]
                other = hidden[:].rearrange("p f t -> p (f t)")[:, 0:FB * n].rearrange("p (f c) -> p f c", f=FB)
                for b in range(FB):
                    bit = (b >> stage) & 1
                    lo, hi = b & ~s, b | s
                    pair = (b >> 1) if stage == 0 else (b & 1)
                    c0 = 8 * stage + 4 * pair + (2 * bit if side == 0 else bit)
                    c1 = c0 + (1 if side == 0 else 2)
                    nc.gpsimd.tensor_scalar(dst[:, b, :], src[:, lo, :], cross_w[:, side, c0:c0 + 1], 0.0,
                                            ALU.mult, ALU.add).then_inc(pool_own, 1)
                    nc.gpsimd.tensor_scalar(other[:, b, :], src[:, hi, :], cross_w[:, side, c1:c1 + 1], 0.0,
                                            ALU.mult, ALU.add).then_inc(pool_own, 1)
                    chain[0] += 2
                pool.wait_ge(pool_own, chain[0])
                ins = nc.gpsimd.tensor_tensor(dst, dst, other, ALU.add)
                if last is not None:
                    ins.then_inc(last, 1)
                    pool.wait_ge(last, 1)
                else:
                    link(ins)

            pool.wait_ge(local_ok, 4)
            cross(1, wcon_sb, 1, down_cross_m[:, 0], None)
            cross(1, down_cross_m[:, 0], 0, down_cross_m[:, 1], downc_ok)
            pool.wait_ge(uplocal_sb, 2)
            cross(0, up_rows, 0, up_cross_m[:, 0], None)
            cross(0, up_cross_m[:, 0], 1, up_cross_m[:, 1], upc_ok)
            link(nc.gpsimd.tensor_tensor(row_ffn[:], row[:, 1, :], row[:, 2, :], ALU.add))
            for b in range(B):
                pool.wait_ge(stats2_ok, b + 1)
                rstd_of(2, slice(b, b + 1), rstd2_ok)
                if b % GB == GB - 1:
                    pool.wait_ge(z2_ok, b + 1)
                    add_row(b // GB, row_ffn[:, None, :], xres2_ok)
                if b in (10, 14):
                    pool.wait_ge(stats3_ok, (b - 10) // GB + 1)
                    rstd_of(3, grp((b - 10) // GB), rstd3_ok)
            for g in range(2, G):
                pool.wait_ge(stats3_ok, g + 1)
                rstd_of(3, grp(g), rstd3_ok)

        @block.vector
        def _(dve):
            chain = [0]

            def link(ins):
                chain[0] += 1
                ins.then_inc(dve_own, 1)
                dve.wait_ge(dve_own, chain[0])

            def norm_stats(src, bs, done):
                for b in range(bs.start, bs.stop):
                    ins = nc.vector.bn_stats(stats[:, b, :], src[:, b, :])
                    ins.then_inc(dve_own, 1)
                    chain[0] += 1
                dve.wait_ge(dve_own, chain[0])
                for b in range(bs.start, bs.stop):
                    ins = nc.vector.bn_aggr(mv[:, b, :], stats[:, b, :])
                    if b < bs.stop - 1:
                        ins.then_inc(dve_own, 1)
                        chain[0] += 1
                dve.wait_ge(dve_own, chain[0])
                ins.then_inc(done, 1)

            nc.vector.memset(v_sb[:, :, :, D:VW], 1.0).then_inc(dve_const, 1)
            nc.vector.memset(decay_row[:], 1.0).then_inc(dve_const, 1)
            dve.wait_ge(dve_const, 2)

            def scale_weights():
                dve.wait_ge(col_in, 16)
                dve.wait_ge(w_in, 16)
                link(nc.vector.tensor_scalar(one_less[:], col[:, C_MIXK:C_MIXK + 3], -1.0, 1.0, ALU.mult, ALU.add))
                for n in range(3):
                    link(nc.vector.tensor_scalar(w_cur[:, n, :], w_sb[:, n, :], col[:, C_MIXK + n:C_MIXK + n + 1], None,
                                                 ALU.mult))
                    ins = nc.vector.tensor_scalar(w_last[:, n, :], w_sb[:, n, :], one_less[:, n:n + 1], None, ALU.mult)
                    if n < 2:
                        link(ins)
                ins.then_inc(mixw_ok, 1)

            def wkv(g):
                e = g % 2
                if g == 0:
                    dve.wait_ge(decay_ok, 1)
                    link(nc.vector.tensor_scalar(decay_row[:], decay_row[:], decay[:, 0:1], None, ALU.mult))
                    link(nc.vector.memset(decay_row[:, :, 0:1], 0.0))
                dr = decay_row[:].rearrange("p b t -> p (b t)")
                dve.wait_ge(ek_ok, g + 1)
                dve.wait_ge(proj_ok, 3 * g + 2)
                if g >= 1:
                    dve.wait_ge(gated_ok, g)
                nc.vector.tensor_tensor(ekv, ek[:, e, :], bank[2][:], ALU.mult).then_inc(ekv_ok, 1)
                link(nc.vector.tensor_tensor_scan(den, dr, ek[:, e, :], 0.0, ALU.mult, ALU.add))
                dve.wait_ge(ekv_ok, g + 1)
                link(nc.vector.tensor_tensor_scan(num, dr, ekv, 0.0, ALU.mult, ALU.add))
                dve.wait_ge(er_ok, g + 1)
                link(nc.vector.scalar_tensor_tensor(den, den, DEN_EPS, er[:, e, :], ALU.add, ALU.mult))
                nc.vector.reciprocal(den, den).then_inc(num_ok, 1)

            def split(s, g, psum, scale, first, rest_s, third):
                p, r = part[s][:, g % 2], rest[:, s, :]
                dve.wait_ge(first, g + 1)
                if g >= 1:
                    dve.wait_ge(third, g)
                nc.vector.scalar_tensor_tensor(r, psum, scale, p[:, 0, :], ALU.mult,
                                               ALU.subtract).then_inc(rest_s, 1)

            def residual1(g):
                dve.wait_ge(y_ok, g + 1)
                nc.vector.tensor_tensor(x_sb[:, grp(g), :], x_sb[:, grp(g), :],
                                        bank[4][:].rearrange("p (b c) -> p b c", b=GB), ALU.add).then_inc(res1_ok, 1)
                dve.wait_ge(res1_ok, g + 1)
                norm_stats(x_sb, grp(g), stats1_ok)

            def mixing_step(s):
                if 0 <= s - 4 < G:
                    dve.wait_ge(q_ok, s - 3)
                    split(0, s - 4, bank[6][:], QK_SCALE, q_first, q_rest, q_third)
                if 0 <= s - 1 < G:
                    wkv(s - 1)
                if 0 <= s - 2 < G:
                    residual1(s - 2)
                if 0 <= s + 2 < G:
                    dve.wait_ge(x_in[s + 2], 16)
                    norm_stats(x_sb, grp(s + 2), stats_ok)
                if s == -2:
                    scale_weights()
                if 0 <= s < G:
                    dve.wait_ge(kc_ok, s + 1)
                    split(1, s, bank[7][:], 1.0, k_first, k_rest, k_third)
                if s == 0:
                    dve.wait_ge(mask_in, 32)
                    for m, b in ((mask_sb, bias_q), (mask_t_sb, bias_k)):
                        link(nc.vector.tensor_scalar(m[:], m[:], -1.0, 1.0, ALU.mult, ALU.add))
                        link(nc.vector.tensor_scalar(b[:], m[:], MASKED, None, ALU.mult))
                    link(nc.vector.tensor_reduce(bias_top[:], bias_q[:], AX.X, ALU.max))
                    nc.vector.tensor_scalar(bias_rel[:], bias_q[:], bias_top[:, 0:1], None,
                                            ALU.subtract).then_inc(bias_ok, 1)
                    link(nc.vector.tensor_copy(bias_part[:, 0, :], bias_k[:]))
                    link(nc.vector.tensor_tensor(bias_rest[:], bias_k[:], bias_part[:, 0, :], ALU.subtract))
                    link(nc.vector.tensor_copy(bias_part[:, 1, :], bias_rest[:]))
                    nc.vector.tensor_tensor(bias_part[:, 2, :], bias_rest[:], bias_part[:, 1, :],
                                            ALU.subtract).then_inc(bias_ok, 1)

            def quad_max(b, q):
                dve.wait_ge(s1_ok, NQ * b + q + 1)
                if q == 0 and b >= 2:
                    dve.wait_ge(shift_ok, b - 1)
                nc.vector.tensor_reduce(top[:, b % 2, q * HQ:(q + 1) * HQ], quads(bank[q % 2][:]), AX.X, ALU.max,
                                        negate=True).then_inc(max_ok, 1)

            def shift_parts(b):
                t = top[:, b % 2, :]
                dve.wait_ge(max_ok, NQ * (b + 1))
                if b >= 1:
                    dve.wait_ge(shiftt_ok, b)
                link(nc.vector.tensor_scalar(shift[:, 0, :], t, bias_top[:, 0:1], None, ALU.subtract))
                link(nc.vector.scalar_tensor_tensor(top_rest[:], t, bias_top[:, 0:1], shift[:, 0, :], ALU.subtract,
                                                    ALU.subtract))
                link(nc.vector.tensor_copy(shift[:, 1, :], top_rest[:]))
                nc.vector.tensor_tensor(shift[:, 2, :], top_rest[:], shift[:, 1, :], ALU.subtract).then_inc(shift_ok, 1)
                dve.wait_ge(shift_ok, b + 1)

            def add_bias(b, q):
                dve.wait_ge(s2_ok, NQ * b + q + 1)
                if b >= 2:
                    dve.wait_ge(av_ok, b - 1)
                nc.vector.tensor_tensor(probs[:, b % 2, q * HQ:(q + 1) * HQ, :], quads(bank[2 + q % 2][:]),
                                        bias_k[:, None, :].to_broadcast([P, HQ, T]), ALU.add).then_inc(added_ok, 1)

            def normalise(b):
                dve.wait_ge(ox_ok, b + 1)
                o = bank[6][:].rearrange("p (h r) -> p h r", r=STRIP)
                nc.vector.reciprocal(rden.rearrange("p (h o) -> p h o", o=1), o[:, :, D:D + 1]).then_inc(rden_ok, 1)
                dve.wait_ge(rden_ok, b + 1)
                if b >= 1:
                    dve.wait_ge(nt_ok, b)
                nc.vector.tensor_tensor(o_norm[:], o[:, :, 0:D],
                                        rden.rearrange("p (h o) -> p h o", o=1).to_broadcast([P, H, D]),
                                        ALU.mult).then_inc(norm_ok, 1)

            def residual2(b):
                dve.wait_ge(op_ok, b + 1)
                if b == 0:
                    dve.wait_ge(xres1_ok, G)
                nc.vector.tensor_tensor(x_sb[:, b, :], xres[:, b, :], bank[6][:, 0:C], ALU.add).then_inc(res2_ok, 1)
                dve.wait_ge(res2_ok, b + 1)
                norm_stats(x_sb, slice(b, b + 1), stats2_ok)

            def residual3(n):
                dve.wait_ge(f_ok, n + 1)
                dve.wait_ge(xres2_ok, n // 2 + 1)
                bs = slice(2 * n, 2 * n + 2)
                nc.vector.tensor_tensor(x_sb[:, bs, :], xres[:, bs, :],
                                        bank[5][:, 0:2 * C].rearrange("p (b c) -> p b c", b=2),
                                        ALU.add).then_inc(res3_ok, 1)

            def output_rows(g):
                dve.wait_ge(rstd3_ok, g + 1)
                for b in range(g * GB, (g + 1) * GB):
                    ins = nc.vector.tensor_scalar(z[:, b, :], x_sb[:, b, :], rstd[:, 3, b:b + 1], nmr[:, 3, b:b + 1],
                                                  ALU.mult, ALU.add)
                    if b < (g + 1) * GB - 1:
                        link(ins)
                ins.then_inc(z3_ok, 1)

            def ffn_stats(g):
                dve.wait_ge(res3_ok, 2 * (g + 1))
                norm_stats(x_sb, grp(g), stats3_ok)

            def attention_step(s):
                for q in range(NQ):
                    if s < B:
                        quad_max(s, q)
                    if 0 <= s - 2 < B and not bias_on_pe(s - 2, q):
                        add_bias(s - 2, q)
                    if q == 0 and 0 <= s - 5 < B:
                        residual2(s - 5)
                    if q == 1 and 0 <= s - 4 < B:
                        normalise(s - 4)
                    if q == 2 and s in (OUT_AT[0], OUT_AT[1]):
                        residual3(2 * OUT_AT.index(s))
                    if q == 0 and s - 1 in (OUT_AT[0], OUT_AT[1]):
                        residual3(2 * OUT_AT.index(s - 1) + 1)
                        ffn_stats(OUT_AT.index(s - 1))
                    if q == 3 and s - 2 in (OUT_AT[0], OUT_AT[1]):
                        output_rows(OUT_AT.index(s - 2))
                if s < B:
                    shift_parts(s)
                if s == DOWN_AT:
                    dve.wait_ge(upc_ok, 1)
                    nc.vector.tensor_tensor(up_b[:], up_cross_m[:, 1, :, C], col[:, C_UPB:C_UPB + FB],
                                            ALU.add).then_inc(upb_sb, 1)
                if s == B + 4:
                    residual3(4)
                if s == B + 5:
                    residual3(5)
                    ffn_stats(2)
            for s in range(-2, G + 1):
                mixing_step(s)
            for s in range(B + 7):
                if s < 3:
                    mixing_step(G + 1 + s)
                attention_step(s)
            output_rows(2)
            residual3(6)
            residual3(7)
            ffn_stats(3)
            output_rows(3)

        @block.scalar
        def _(act):
            act.wait_ge(col_in, 16)
            nc.scalar.activation(decay[:], col[:, C_DECAY:C_DECAY + 1], ACT.Exp).then_inc(decay_ok, 1)

            def apply_norm(k, bs, ready, n, done):
                act.wait_ge(ready, n)
                for b in range(bs.start, bs.stop):
                    nc.scalar.activation(z[:, b, :], x_sb[:, b, :], ACT.Identity, bias=nmr[:, k, b:b + 1],
                                         scale=rstd[:, k, b:b + 1]).then_inc(done, 1)

            def second_part(s, g, rest_s, done):
                act.wait_ge(rest_s, g + 1)
                nc.scalar.activation(part[s][:, g % 2, 1, :], rest[:, s, :], ACT.Copy).then_inc(done, 1)

            def mixing_step(s):
                if 0 <= s < G:
                    act.wait_ge(t0_ok, s + 1)
                    if s == 0:
                        act.wait_ge(const_ok, 3)
                    if s >= 2:
                        act.wait_ge(proj_ok, 3 * (s - 1))
                    nc.scalar.activation(xn[:, s % 2, :, 1:T + 1], bank[0][:].rearrange("p (b t) -> p b t", b=GB),
                                         ACT.Identity, bias=col[:, C_B:C_B + 1],
                                         scale=col[:, C_G:C_G + 1]).then_inc(xn_ok, 1)
                if 0 <= s < G:
                    act.wait_ge(vc_ok, s + 1)
                    if s == 0:
                        act.wait_ge(dve_const, 2)
                    nc.scalar.activation(v_sb[:, grp(s), :, 0:D],
                                         bank[5][:].rearrange("p (b h d) -> p b h d", b=GB, h=H),
                                         ACT.Copy).then_inc(v_ok, 1)
                if 0 <= s - 4 < G:
                    second_part(0, s - 4, q_rest, q_second)
                if 0 <= s + 1 < G:
                    apply_norm(0, grp(s + 1), rstd_ok, s + 2, z0_ok)
                if 0 <= s - 3 < G:
                    apply_norm(1, grp(s - 3), rstd1_ok, s - 2, z1_ok)
                if 0 <= s - 1 < G:
                    second_part(1, s - 1, k_rest, k_second)
                if 0 <= s < G:
                    act.wait_ge(proj_ok, 3 * s + 1)
                    if s >= 2:
                        act.wait_ge(gated_ok, s - 1)
                    nc.scalar.activation(ek[:, s % 2, :], bank[1][:], ACT.Exp).then_inc(ek_ok, 1)
                    act.wait_ge(proj_ok, 3 * s + 3)
                    nc.scalar.activation(er[:, s % 2, :], bank[3][:], ACT.Exp, scale=-1.0).then_inc(er_raw, 1)
                if 0 <= s - 3 < G:
                    act.wait_ge(t1_ok, s - 2)
                    nc.scalar.activation(zt[:, (s - 3) % 2, :], bank[5][:], ACT.Copy).then_inc(zt1_ok, 1)
                if 0 <= s < G:
                    act.wait_ge(er_raw, s + 1)
                    nc.scalar.activation(er[:, s % 2, :], er[:, s % 2, :], ACT.Identity,
                                         bias=one_col[:, 0:1]).then_inc(er_ok, 1)
                    act.wait_ge(kc_ok, s + 1)
                    if s >= 2:
                        act.wait_ge(spilled[1][s - 2], 16)
                    nc.scalar.activation(part[1][:, s % 2, 0, :], bank[7][:], ACT.Copy).then_inc(k_first, 1)
                if 0 <= s - 3 < G:
                    g = s - 3
                    act.wait_ge(q_ok, g + 1)
                    if g >= 2:
                        act.wait_ge(spilled[0][g - 2], 16)
                    nc.scalar.activation(part[0][:, g % 2, 0, :], bank[6][:], ACT.Copy,
                                         scale=QK_SCALE).then_inc(q_first, 1)

            def exps(b, q):
                p = probs[:, b % 2, q * HQ:(q + 1) * HQ, :]
                if bias_on_pe(b, q):
                    act.wait_ge(s2_ok, NQ * b + q + 1)
                    if b >= 2:
                        act.wait_ge(av_ok, b - 1)
                    src = quads(bank[2 + q % 2][:])
                else:
                    act.wait_ge(added_ok, added_before(b, q) + 1)
                    src = p
                nc.scalar.activation(p, src, ACT.Exp).then_inc(exp_ok, 1)

            def shift_copy(b):
                act.wait_ge(shiftt_ok, b + 1)
                if b >= 2:
                    act.wait_ge(shift_in[b % 2], 48 * (b // 2))
                nc.scalar.activation(shift_t[:, b % 2, :], bank[7][0:NS * H, 0:T // 2].bitcast(BF16),
                                     ACT.Copy).then_inc(shiftt_sb, 1)

            def copy_out(ready, n, dst, src, done):
                act.wait_ge(ready, n)
                nc.scalar.activation(dst, src, ACT.Copy).then_inc(done, 1)

            def hidden_copy(g, f):
                act.wait_ge(h_ok, FB * g + f + 1)
                if f == 0:
                    act.wait_ge(upb_sb, 1)
                    if g >= 1:
                        act.wait_ge(f_ok, 2 * g)
                nc.scalar.activation(hidden[:, f, :], bank[5][:], ACT.Identity,
                                     bias=up_b[:, f:f + 1]).then_inc(h_sb, 1)

            def attention_step(s):
                for q in range(NQ):
                    if q == 0 and 0 <= s - 4 < B:
                        act.wait_ge(av_ok, s - 3)
                        if s - 4 >= 1:
                            act.wait_ge(ox_ok, s - 4)
                        nc.scalar.activation(o_t[:].rearrange("p g t -> p (g t)"), bank[4][:],
                                             ACT.Copy).then_inc(ot_ok, 1)
                    if q == 1 and 0 <= s - 1 < B:
                        shift_copy(s - 1)
                    if 0 <= s - 2 < B:
                        exps(s - 2, q)
                    if q == 1 and s == UP_AT:
                        act.wait_ge(y_ok, G)
                        copy_out(uplocal_ok, 1, up_rows[:, :, 0:C], bank[5][:].rearrange("p (f c) -> p f c", f=FB),
                                 uplocal_sb)
                    if q == 3 and s == UP_AT:
                        copy_out(uplocal_ok, 2, up_rows[:, :, C], bank[5][:, 0:FB], uplocal_sb)
                    if q == 1 and s == DOWN_AT:
                        copy_out(downm_ok, 1, down_m.rearrange("p f c -> p (f c)"), bank[5][:], downm_sb)
                    if q == 3 and s == DOWN_AT:
                        copy_out(upt_ok, 1, up_m.rearrange("p f c -> p (f c)"), bank[5][:], upm_ok)
                    for g in range(2):
                        if q % 2 == 1 and s - HIDDEN_AT[g] in (0, 1):
                            hidden_copy(g, 2 * (s - HIDDEN_AT[g]) + q // 2)
                    if q == 2 and 0 <= s - 7 < B:
                        b = s - 7
                        if b >= 2 * GB:
                            act.wait_ge(h_ok, FB * (b // GB - 1))
                        copy_out(t2_ok, b + 1, zt[:, (b // GB) % 2, b % GB * T:(b % GB + 1) * T], bank[7][:, 0:T],
                                 zt2_ok)
                    if q == 3 and 0 <= s - 4 < B:
                        if s - 4 >= 1:
                            act.wait_ge(op_ok, s - 4)
                        copy_out(nt_ok, s - 3, o_norm_t[:], bank[7][:, 0:T], ntsb_ok)
                if 0 <= s - 6 < B:
                    apply_norm(2, slice(s - 6, s - 5), rstd2_ok, s - 5, z2_ok)
                for g in range(2):
                    if s == HIDDEN_AT[g] + 2:
                        act.wait_ge(h_sb, FB * (g + 1))
                        nc.scalar.activation(hidden[:], hidden[:], ACT.Gelu).then_inc(gelu_ok, FB)
                if s in (B + 3, B + 6):
                    g = 2 if s == B + 3 else 3
                    for f in range(FB):
                        act.wait_ge(h_ok, FB * g + f + 1)
                        if f == 0:
                            act.wait_ge(f_ok, 2 * g)
                        nc.scalar.activation(hidden[:, f, :], bank[f][:], ACT.Gelu,
                                             bias=up_b[:, f:f + 1]).then_inc(gelu_ok, 1)

            for s in range(-1, G + 1):
                mixing_step(s)
            for s in range(B + 7):
                if s < 3:
                    mixing_step(G + 1 + s)
                attention_step(s)

        @block.tensor
        def _(pe):
            def mm(out_, lhs, rhs, start=True, stop=True, **kw):
                return nc.tensor.matmul(out_, lhs, rhs, start=start, stop=stop, **kw)

            def transposes(dst, g):
                for t in range(GB):
                    ins = nc.tensor.transpose(dst[:, t * T:(t + 1) * T], z[:, g * GB + t, :], ident[:])
                return ins

            def project_in(g):
                pe.wait_ge(z0_ok, GB * (g + 1))
                if g >= 1:
                    pe.wait_ge(xn_ok, g)
                transposes(bank[0], g).then_inc(t0_ok, 1)
                pe.wait_ge(ctx_in[g], 16)
                if g >= 1:
                    pe.wait_ge(v_ok, g)
                if g >= 4:
                    pe.wait_ge(zt1_ok, g - 3)
                for t in range(GB):
                    ins = mm(bank[5][:, t * C:(t + 1) * C], ctx_sb[:, g % 2, t * T:(t + 1) * T], w_sb[:, X_V, :])
                ins.then_inc(vc_ok, 1)
                pe.wait_ge(xn_ok, g + 1)
                pe.wait_ge(mixw_ok, 1)
                for n, (free, w) in enumerate(((ek_ok, W_K), (ekv_ok, W_V), (er_raw, W_R))):
                    if g >= 1:
                        pe.wait_ge(free, g)
                    dst = bank[1 + n][:].rearrange("p (b t) -> p b t", b=GB)
                    mm(dst, w_cur[:, w, :], xn[:, g % 2, :, 1:T + 1], stop=False)
                    mm(dst, w_last[:, w, :], xn[:, g % 2, :, 0:T], start=False).then_inc(proj_ok, 1)

            def keys(g):
                if g >= 1:
                    pe.wait_ge(k_rest, g)
                mm(bank[7][:], w_sb[:, X_K, :], ctx_sb[:, g % 2, :]).then_inc(kc_ok, 1)

            def project_out(g):
                pe.wait_ge(gated_ok, g + 1)
                if g >= 1:
                    pe.wait_ge(res1_ok, g)
                for t in range(GB):
                    ins = mm(bank[4][:, t * C:(t + 1) * C], gated[:, g % 2, t * T:(t + 1) * T], w_sb[:, W_O, :])
                ins.then_inc(y_ok, 1)

            def turn_queries(g):
                pe.wait_ge(z1_ok, GB * (g + 1))
                pe.wait_ge(v_ok, min(g + 4, G))
                if g >= 1:
                    pe.wait_ge(zt1_ok, g)
                transposes(bank[5], g).then_inc(t1_ok, 1)

            def project_q(g):
                pe.wait_ge(zt1_ok, g + 1)
                if g >= 1:
                    pe.wait_ge(q_rest, g)
                mm(bank[6][:], w_sb[:, X_Q, :], zt[:, g % 2, :]).then_inc(q_ok, 1)

            up_l = local_m[0][(LOCAL - 1) % 2][:].rearrange("p (f j) -> p f j", f=FB)
            down_l = local_m[1][0][:].rearrange("p (f j) -> p f j", f=FB)
            pe.wait_ge(ident_ok, 2)
            pe.wait_ge(w_in, 16)

            def mixing_step(s):
                if 0 <= s < G:
                    project_in(s)
                if 0 <= s - 3 < G:
                    turn_queries(s - 3)
                if 0 <= s < G:
                    keys(s)
                if 0 <= s - 3 < G:
                    project_q(s - 3)
                if 0 <= s - 1 < G:
                    project_out(s - 1)

            def scores(b, q):
                g = b // GB
                if b % GB == 0 and q == 0:
                    for s in range(2):
                        pe.wait_ge(stack_in[s][g % 2], 16 * len(RUNS[s]) * (g // 2 + 1))
                        if g == 1:
                            pe.wait_ge(pad_in[s], 16)
                    if g >= 2:
                        pe.wait_ge(stack_zero[g % 2], 16 * (g // 2))
                if NQ * b + q >= 2:
                    pe.wait_ge(max_ok, NQ * b + q - 1)
                mm(quads(bank[q % 2][:]), ident_bf[:], bias_rel[:, None, :].to_broadcast([P, HQ, T]), stop=False,
                   skip_group_check=True)
                for j in range(HQ):
                    h = HQ * q + j
                    ins = mm(bank[q % 2][:, j * T:(j + 1) * T], head_tok(0, b, h), head_tok(1, b, h), start=False,
                             stop=(j == HQ - 1), skip_group_check=True)
                ins.then_inc(s1_ok, 1)

            def scores_t(b, q):
                if q == 0:
                    pe.wait_ge(shift_in[b % 2], 48 * (b // 2 + 1))
                n = NQ * b + q - 2
                if n < 0:
                    pe.wait_ge((ekv_ok, er_raw)[q], G)
                elif bias_on_pe(n // NQ, n % NQ):
                    pe.wait_ge(exp_ok, n + 1)
                else:
                    pe.wait_ge(added_ok, added_before(n // NQ, n % NQ) + 1)
                if bias_on_pe(b, q):
                    for i in range(3):
                        mm(quads(bank[2 + q % 2][:]), ident_bf[:], bias_part[:, i, None, :].to_broadcast([P, HQ, T]),
                           start=(i == 0), stop=False, skip_group_check=True)
                for j in range(HQ):
                    h = HQ * q + j
                    if bias_on_pe(b, q):
                        ins = mm(bank[2 + q % 2][:, j * T:(j + 1) * T], head_tok(1, b, h), head_tok(0, b, h),
                                 start=False, stop=(j == HQ - 1), skip_group_check=True)
                    else:
                        ins = mm(bank[2 + q % 2][:, j * T:(j + 1) * T], head_tok(1, b, h), head_tok(0, b, h))
                ins.then_inc(s2_ok, 1)

            def values(b, q):
                pe.wait_ge(exp_ok, NQ * b + q + 1)
                if q == 0 and b == 0:
                    pe.wait_ge(res1_ok, G)
                if q == 0 and b >= 1:
                    pe.wait_ge(ot_ok, b)
                for j in range(HQ):
                    h = HQ * q + j
                    ins = mm(bank[4][STRIP * j:STRIP * j + VW, q * T:(q + 1) * T], v_sb[:, b, h, :],
                             probs[:, b % 2, h, :])
                if q == NQ - 1:
                    ins.then_inc(av_ok, 1)

            def hidden_part(g, f, dst):
                pe.wait_ge(zt2_ok, GB * (g + 1))
                mm(dst[:], up_m[:, f, :], zt[:, g % 2, :]).then_inc(h_ok, 1)

            def ffn_out(n):
                g = n // 2
                pe.wait_ge(gelu_ok, FB * (g + 1))
                if n >= 1:
                    pe.wait_ge(res3_ok, n)
                for t in range(2):
                    at = (n % 2 * 2 + t) * T
                    for f in range(FB):
                        ins = mm(bank[5][:, t * C:(t + 1) * C], hidden[:, f, at:at + T], down_m[:, f, :],
                                 start=(f == 0), stop=(f == FB - 1))
                ins.then_inc(f_ok, 1)

            def beside(s, q):
                if s == UP_AT and q == 1:
                    pe.wait_ge(local_ok, 2)
                    pe.wait_ge(zt1_ok, G)
                    pe.wait_ge(v_ok, G)
                    for f in range(FB):
                        ins = mm(bank[5][:, f * C:(f + 1) * C], up_l[:, f, :], wexp_sb[:, f, 0:C])
                    ins.then_inc(uplocal_ok, 1)
                if s == UP_AT and q == 3:
                    pe.wait_ge(uplocal_sb, 1)
                    for f in range(FB):
                        ins = mm(bank[5][:, f:f + 1], up_l[:, f, :], wexp_sb[:, f, C:C + 1])
                    ins.then_inc(uplocal_ok, 1)
                if s == DOWN_AT and q == 1:
                    pe.wait_ge(uplocal_sb, 2)
                    pe.wait_ge(local_ok, 4)
                    pe.wait_ge(downc_ok, 1)
                    for f in range(FB):
                        ins = mm(bank[5][:, f * C:(f + 1) * C], down_l[:, f, :], down_cross_m[:, 1, f, :])
                    ins.then_inc(downm_ok, 1)
                if s == DOWN_AT and q == 3:
                    pe.wait_ge(downm_sb, 1)
                    pe.wait_ge(upc_ok, 1)
                    for f in range(FB):
                        ins = nc.tensor.transpose(bank[5][:, f * P:(f + 1) * P], up_cross_m[:, 1, f, 0:C], ident[:])
                    ins.then_inc(upt_ok, 1)
                for g in range(2):
                    if s - HIDDEN_AT[g] in (0, 1) and q % 2 == 1:
                        f = 2 * (s - HIDDEN_AT[g]) + q // 2
                        if f == 0 and g == 0:
                            pe.wait_ge(upm_ok, 1)
                        elif f == 0:
                            pe.wait_ge(res3_ok, 2 * g)
                        else:
                            pe.wait_ge(h_sb, FB * g + f)
                        hidden_part(g, f, bank[5])
                    if s == OUT_AT[g] and q % 2 == 1:
                        ffn_out(2 * g + q // 2)

            def attention_step(s):
                for q in range(NQ):
                    if s < B:
                        scores(s, q)
                    if q == 0 and 0 <= s - 5 < B:
                        pe.wait_ge(ntsb_ok, s - 4)
                        pe.wait_ge(norm_ok, s - 4)
                        mm(bank[6][:, 0:C], o_norm_t[:], w_sb[:, X_O, :]).then_inc(op_ok, 1)
                    if q == 1 and 0 <= s - 4 < B:
                        pe.wait_ge(ot_ok, s - 3)
                        if s - 4 == 0:
                            pe.wait_ge(q_rest, G)
                        else:
                            pe.wait_ge(res2_ok, s - 4)
                        for n in range(NQ):
                            ins = nc.tensor.transpose(bank[6][:, n * T:(n + 1) * T], o_t[:, n, :], ident[:])
                        ins.then_inc(ox_ok, 1)
                    if q == 2 and 0 <= s - 7 < B:
                        pe.wait_ge(z2_ok, s - 6)
                        pe.wait_ge(shiftt_sb, min(s, B))
                        pe.wait_ge(ntsb_ok, min(s - 4, B))
                        nc.tensor.transpose(bank[7][:, 0:T], z[:, s - 7, :], ident[:]).then_inc(t2_ok, 1)
                    if 0 <= s - 2 < B:
                        scores_t(s - 2, q)
                    if q == 0 and 0 <= s - 1 < B:
                        pe.wait_ge(shift_ok, s)
                        if s == 1:
                            pe.wait_ge(k_rest, G)
                        if s - 5 >= 0:
                            pe.wait_ge(ntsb_ok, s - 4)
                        nc.tensor.transpose(bank[7][0:NS * H, 0:T // 2].bitcast(BF16),
                                            shift[:].rearrange("p n h -> p (n h)"), ident_bf[:]).then_inc(shiftt_ok, 1)
                    if 0 <= s - 3 < B:
                        values(s - 3, q)
                    if q == 3 and 0 <= s - 4 < B:
                        pe.wait_ge(norm_ok, s - 3)
                        pe.wait_ge(shiftt_sb, min(s, B))
                        if s - 7 >= 0:
                            pe.wait_ge(zt2_ok, s - 6)
                        nc.tensor.transpose(bank[7][:, 0:T], o_norm[:].rearrange("p h d -> p (h d)"),
                                            ident[:]).then_inc(nt_ok, 1)
                    beside(s, q)
                if s in (B + 3, B + 6):
                    g = 2 if s == B + 3 else 3
                    for f in range(FB):
                        if g == 2:
                            pe.wait_ge(max_ok, NQ * B)
                            pe.wait_ge(exp_ok, NQ * B)
                        else:
                            pe.wait_ge(gelu_ok, FB * (g - 1) + f + 1)
                        hidden_part(g, f, bank[f])
                    if g == 3:
                        ffn_out(6)
                        ffn_out(7)
                if s == B + 4:
                    ffn_out(4)
                if s == B + 5:
                    ffn_out(5)

            for s in range(G + 1):
                mixing_step(s)
            pe.wait_ge(bias_ok, 2)
            pe.wait_ge(dve_const, 2)
            pe.wait_ge(xn_ok, G)
            pe.wait_ge(ek_ok, G)
            for s in range(B + 7):
                attention_step(s)
                if s < 3:
                    mixing_step(G + 1 + s)


def kernel(**inputs):
    import numpy as np
    import concourse.bacc as bacc
    from concourse.bass_utils import run_bass_kernel_spmd

    def f(name):
        return np.asarray(inputs[name])

    P, FB, LOCAL = 128, 4, 7
    x = f("x")
    attn = {n: f("L0_attn_" + n) for n in ("time_decay", "time_mix_k", "time_mix_v", "time_mix_r",
                                           "Wk", "Wv", "Wr", "Wo", "ln_g", "ln_b")}

    def by_dim(w):
        return w.reshape(P, 16, 8).transpose(0, 2, 1).reshape(P, P)

    weights = np.stack([attn["Wk"].T, attn["Wv"].T, attn["Wr"].T, attn["Wo"].T,
                        by_dim(f("L0_xattn_Wq")), by_dim(f("L0_xattn_Wk")), f("L0_xattn_Wv"), f("L0_xattn_Wo")], axis=1)
    columns = np.concatenate(
        [attn[n].reshape(P, 1) for n in ("time_decay", "time_mix_k", "time_mix_v", "time_mix_r", "ln_g", "ln_b")]
        + [f("L0_ffn_up_bias").reshape(FB, P).T], axis=1)
    rows = np.stack([f("L0_xattn_bo"), f("L0_ffn_b_con"), f("L0_ffn_down_bias")])
    w_exp_t = np.concatenate([f("L0_ffn_W_exp").T.reshape(FB, P, P), f("L0_ffn_b_exp").reshape(FB, P, 1)],
                             axis=2).transpose(1, 0, 2)
    w_con = f("L0_ffn_W_con").reshape(FB, P, P).transpose(1, 0, 2)

    def up_local(w):
        p, blk = np.arange(P)[:, None, None, None], np.arange(FB)[None, :, None, None]
        parts = []
        for k in range(LOCAL):
            bit, low = np.arange(2)[None, None, :, None], np.arange(2 ** k)[None, None, None, :]
            pair = ((blk * P + p) >> (k + 1) << k) + low
            parts.append(w[k][pair, bit, (p >> k) & 1].reshape(P, -1))
        return np.concatenate(parts, axis=1)

    def down_local(w):
        p, blk = np.arange(P)[:, None, None, None], np.arange(FB)[None, :, None, None]
        parts = []
        for k in range(LOCAL - 1, -1, -1):
            n = 2 ** (LOCAL - 1 - k)
            high, bit = np.arange(n)[None, None, :, None], np.arange(2)[None, None, None, :]
            pair = ((blk * n + high) << k) + (p & (2 ** k - 1))
            parts.append(w[k][pair, (p >> k) & 1, bit].reshape(P, -1))
        return np.concatenate(parts, axis=1)

    def cross(w):
        return np.stack([w[k].reshape(2, P, 2, 2).transpose(1, 0, 2, 3) for k in (LOCAL, LOCAL + 1)],
                        axis=1).reshape(P, 16)

    up, down = f("L0_ffn_up_weights"), f("L0_ffn_down_weights")
    mask = f("mask_1x1xSxS2_fk0")[0, 0]
    arrays = {
        "x": x, "ctx_t": f("ctx_1024").transpose(2, 0, 1).reshape(P, -1), "mask": mask, "mask_t": mask.T,
        "weights": weights, "columns": columns, "rows": rows, "w_exp_t": w_exp_t, "w_con": w_con,
        "up_local": up_local(up), "down_local": down_local(down), "up_cross": cross(up), "down_cross": cross(down),
    }
    nc = bacc.Bacc("TRN2", target_bir_lowering=False, num_devices=1)
    given, args = {}, []
    for name, a in arrays.items():
        a = np.ascontiguousarray(a)
        given[f"in_{name}"] = a
        args.append(nc.dram_tensor(f"in_{name}", a.shape, mybir.dt.from_np(a.dtype), kind="ExternalInput").ap())
    args.append(nc.dram_tensor("out_y", x.shape, FP32, kind="ExternalOutput").ap())
    decoder_program(nc, *args)
    r = run_bass_kernel_spmd(nc, [given], core_ids=[0])
    return r.results[0]["out_y"]
```

```python
from contextlib import ExitStack

import concourse.bass as bass
from concourse import mybir

FP32 = mybir.dt.float32
BF16 = mybir.dt.bfloat16
ALU = mybir.AluOpType
ACT = mybir.ActivationFunctionType
AX = mybir.AxisListType


def decoder_program(nc, x, ctx_t, mask, mask_t, weights, columns, rows, w_exp_t, w_con,
                    up_local, down_local, up_cross, down_cross, out):
    P = 128
    B = x.shape[0]
    C = x.shape[2]
    T = x.shape[1]
    GB = 4
    G = B // GB
    GT = GB * T
    H = 16
    D = C // H
    HQ = 4
    NQ = H // HQ
    VW = D + 1
    STRIP = 32
    FB = w_exp_t.shape[1]
    LOCAL = 7
    EPS = 1e-5
    DEN_EPS = 1e-8
    MASKED = -1000000000.0
    QK_SCALE = float(D) ** -0.5
    PAIRS = [(0, 0), (0, 1), (0, 2), (1, 0), (1, 1), (2, 0)]
    RUNS = [(0, 3), (3, 2), (5, 1)]
    SHIFT_ROW = len(PAIRS) * D
    NS = 3
    SK = 96
    C_DECAY, C_MIXK, C_MIXV, C_MIXR, C_G, C_B, C_UPB = range(7)
    W_K, W_V, W_R, W_O, X_Q, X_K, X_V, X_O = range(8)

    NP = B // 2

    UP_AT = 3
    DOWN_AT = 8
    HIDDEN_AT = {(10, 0): (0, 0), (10, 3): (0, 1), (11, 1): (0, 2), (11, 3): (0, 3),
                 (14, 2): (1, 0), (15, 0): (1, 1), (15, 2): (1, 2), (16, 0): (1, 3)}
    GELU_AT = {(12, 0): 0, (18, 0): 1}
    DIRECT_AT = {(17, 3): (2, (0, 1), (0, GT)), (18, 0): (2, (2, 3), (0, GT)), (19, 3): (3, range(FB), (0, GT // 2))}
    DIRECT_GELU_AT = {(18, 0): (2, (0, GT)), (19, 3): (3, (0, GT // 2))}
    OUT_AT = {(13, 2): 0, (13, 3): 1, (18, 1): 2, (18, 3): 3, (19, 2): 4, (20, 0): 5, (20, 3): 6}
    RES_AT = {(13, 2): 0, (14, 0): 1, (18, 2): 2, (19, 0): 3, (19, 2): 4, (20, 1): 5}
    ROWS_AT = {(14, 2): 0, (15, 2): 1, (19, 2): 2, (20, 1): 3, (20, 2): 4, (21, 1): 5}

    PE_QUADS = (3,)

    ctx = ExitStack()
    with ctx:
        def sb(name, shape, dt=FP32):
            return ctx.enter_context(nc.sbuf_tensor(name, shape, dt))

        def sem(name):
            return ctx.enter_context(nc.semaphore(name))

        w_sb = sb("w_sb", [P, 8, C])
        col = sb("col", [P, columns.shape[1]])
        row = sb("row", [P, 3, C])
        row_ffn = sb("row_ffn", [P, C])
        ident = sb("ident", [P, P])
        ident_bf = sb("ident_bf", [P, P], BF16)
        one_col = sb("one_col", [P, 1])
        one_less = sb("one_less", [P, 3])
        neg_half = sb("neg_half", [P, GB])
        decay = sb("decay", [P, 1])
        decay_row = sb("decay_row", [P, GB, T])
        mask_sb = sb("mask_sb", [P, T])
        mask_t_sb = sb("mask_t_sb", [P, T])
        bias_q = sb("bias_q", [P, T])
        bias_top = sb("bias_top", [P, 1])
        bias_rel = sb("bias_rel", [P, T], BF16)
        bias_k = sb("bias_k", [P, T])
        bias_part = sb("bias_part", [P, 3, T], BF16)
        bias_rest = sb("bias_rest", [P, T])

        x_sb = sb("x_sb", [P, B, C])
        xres = sb("xres", [P, B, C])
        ctx_sb = sb("ctx_sb", [P, 2, GT])
        stats = sb("stats", [P, B, 6])
        mv = sb("mv", [P, B, 2])
        rstd = sb("rstd", [P, 4, B])
        nmr = sb("nmr", [P, 4, B])
        z = sb("z", [P, B, C])
        xn = sb("xn", [P, 2, GB, T + 1])
        exps_kr = sb("exps_kr", [P, 4, GT])
        ek, er = exps_kr[:, 0:2, :], exps_kr[:, 2:4, :]
        hidden = [sb("hidden", [P, FB, GT]), exps_kr]
        w_cur = sb("w_cur", [P, 3, C])
        w_last = sb("w_last", [P, 3, C])
        early = sb("early", [P, 5, GT])
        ekv, den, num, gated = early[:, 0, :], early[:, 1, :], early[:, 2, :], early[:, 3:5, :]
        zt = sb("zt", [P, 2, GT])
        part = [sb(f"part_{s}", [P, 2, 3, GT], BF16) for s in "qk"]
        rest = sb("rest", [P, 2, GT])
        stack = [sb(f"stack_{s}", [P, 2, H, GT], BF16) for s in "qk"]
        v_sb = sb("v_sb", [P, B, H, VW])
        probs = sb("probs", [P, 2, H, T])
        top = sb("top", [P, 2, H])
        top_rest = sb("top_rest", [P, H])
        shift = sb("shift", [P, NS, H], BF16)
        shift_t = sb("shift_t", [NS * H, 2, T], BF16)
        o_t = sb("o_t", [P, NQ, T])
        rden = sb("rden", [P, H])
        o_norm = sb("o_norm", [P, H, D])
        o_norm_t = sb("o_norm_t", [P, T])
        wexp_sb = sb("wexp_sb", [P, FB, C + 1])
        wcon_sb = sb("wcon_sb", [P, FB, C])
        n_local = FB * (2 ** (LOCAL + 1) - 2)
        local_w = sb("local_w", [P, 2, 2 * FB * (C + 1)])
        local_m = [[sb(f"local_m{s}{i}", [P, FB * P >> i]) for i in range(2)] for s in range(2)]
        cross_w = sb("cross_w", [P, 2, 16])
        early_flat = early[:].rearrange("p n t -> p (n t)")
        up_rows = early_flat[:, 0:FB * (C + 1)].rearrange("p (f c) -> p f c", f=FB)
        up_cross_m = local_w[:, 0, :].rearrange("p (n f c) -> p n f c", n=2, f=FB)
        down_cross_m = local_w[:, 1, 0:2 * FB * C].rearrange("p (n f c) -> p n f c", n=2, f=FB)
        up_m = early_flat[:, 2 * GT:3 * GT].rearrange("p (f c) -> p f c", f=FB)
        down_m = early_flat[:, 3 * GT:4 * GT].rearrange("p (f c) -> p f c", f=FB)
        up_b = sb("up_b", [P, FB])

        spill = [nc.dram_tensor(f"spill_{s}", [G, 3, P, GT], BF16, kind="Internal").ap() for s in "qk"]

        bank = [ctx.enter_context(nc.psum_tensor(f"bank{i}", [P, 512], FP32)) for i in range(8)]

        w_in, col_in, row_in, mask_in, ffn_in = [sem(n) for n in ("w_in", "col_in", "row_in", "mask_in", "ffn_in")]
        x_in = [sem(f"x_in{g}") for g in range(G)]
        ctx_in = [sem(f"ctx_in{g}") for g in range(G)]
        ident_0 = sem("ident_0")
        ident_ok = sem("ident_ok")
        const_ok = sem("const_ok")
        dve_const = sem("dve_const")
        decay_ok = sem("decay_ok")
        bias_ok = sem("bias_ok")
        dve_own = sem("dve_own")
        pool_own = sem("pool_own")
        stats_ok = sem("stats_ok")
        rstd_ok = sem("rstd_ok")
        z0_ok = sem("z0_ok")
        t0_ok = sem("t0_ok")
        xn_ok = sem("xn_ok")
        mixw_ok = sem("mixw_ok")
        proj_ok = sem("proj_ok")
        ek_ok = sem("ek_ok")
        er_raw = sem("er_raw")
        er_ok = sem("er_ok")
        ekv_ok = sem("ekv_ok")
        num_ok = sem("num_ok")
        gated_ok = sem("gated_ok")
        y_ok = sem("y_ok")
        res1_ok = sem("res1_ok")
        stats1_ok = sem("stats1_ok")
        rstd1_ok = sem("rstd1_ok")
        z1_ok = sem("z1_ok")
        xres1_ok = sem("xres1_ok")
        t1_ok = sem("t1_ok")
        zt1_ok = sem("zt1_ok")
        q_ok = sem("q_ok")
        q_first = sem("q_first")
        q_rest = sem("q_rest")
        q_second = sem("q_second")
        q_third = sem("q_third")
        kc_ok = sem("kc_ok")
        k_first = sem("k_first")
        k_rest = sem("k_rest")
        k_second = sem("k_second")
        k_third = sem("k_third")
        vc_ok = sem("vc_ok")
        v_ok = sem("v_ok")
        stack_in = [[sem(f"stack_{s}_in{i}") for i in range(2)] for s in "qk"]
        spilled = [[sem(f"spilled_{s}{g}") for g in range(G)] for s in "qk"]
        stack_zero = [sem(f"stack_zero{i}") for i in range(2)]
        stack_filled = [sem(f"stack_{s}_filled") for s in "qk"]
        pad_in = [sem(f"pad_{s}_in") for s in "qk"]
        s1_ok = sem("s1_ok")
        max_ok = sem("max_ok")
        shift_step = sem("shift_step")
        shift_ok = sem("shift_ok")
        shiftt_ok = sem("shiftt_ok")
        shiftt_sb = sem("shiftt_sb")
        shift_in = [sem(f"shift_in{i}") for i in range(2)]
        s2_ok = sem("s2_ok")
        added_ok = sem("added_ok")
        exp_ok = sem("exp_ok")
        av_ok = sem("av_ok")
        ot_ok = sem("ot_ok")
        ox_ok = sem("ox_ok")
        rden_ok = sem("rden_ok")
        norm_ok = sem("norm_ok")
        nt_ok = sem("nt_ok")
        ntsb_ok = sem("ntsb_ok")
        op_ok = sem("op_ok")
        res2_ok = sem("res2_ok")
        row_stats_ok = sem("row_stats_ok")
        stats2_ok = sem("stats2_ok")
        rstd2_ok = sem("rstd2_ok")
        z2_ok = sem("z2_ok")
        xres2_ok = sem("xres2_ok")
        local_ok = sem("local_ok")
        uplocal_ok = sem("uplocal_ok")
        uplocal_sb = sem("uplocal_sb")
        upc_ok = sem("upc_ok")
        upt_ok = sem("upt_ok")
        upm_ok = sem("upm_ok")
        upb_sb = sem("upb_sb")
        downc_ok = sem("downc_ok")
        downm_ok = sem("downm_ok")
        downm_sb = sem("downm_sb")
        t2_ok = sem("t2_ok")
        zt2_ok = sem("zt2_ok")
        h_ok = sem("h_ok")
        h_sb = sem("h_sb")
        gelu_ok = sem("gelu_ok")
        f_ok = sem("f_ok")
        res3_ok = sem("res3_ok")
        stats3_ok = sem("stats3_ok")
        rstd3_ok = sem("rstd3_ok")
        z3_ok = sem("z3_ok")
        out_done = sem("out_done")

        def tok(g):
            return slice(g * GT, (g + 1) * GT)

        def grp(g):
            return slice(g * GB, (g + 1) * GB)

        def pair(n):
            return slice(2 * n, 2 * n + 2)

        def head_tok(s, b, h):
            g, t = divmod(b, GB)
            return stack[s][0:SK, g % 2, h, t * T:(t + 1) * T]

        def bias_on_pe(b, q):
            return q in PE_QUADS

        def added_before(b, q):
            return sum(not bias_on_pe(*divmod(n, NQ)) for n in range(NQ * b + q))

        def quads(ap):
            return ap.rearrange("p (h t) -> p h t", h=HQ)

        block = ctx.enter_context(nc.Block())

        @block.sync
        def _(sp):
            def load(dst, src, s):
                sp.dma_start(dst, src).then_inc(s, 16)

            x_tok = x.rearrange("b t c -> t b c")
            load(x_sb[:, grp(0), :], x_tok[:, grp(0), :], x_in[0])
            load(col[:], columns, col_in)
            load(w_sb[:], weights, w_in)
            load(ctx_sb[:, 0, :], ctx_t[:, tok(0)], ctx_in[0])
            load(x_sb[:, grp(1), :], x_tok[:, grp(1), :], x_in[1])
            load(mask_sb[:], mask, mask_in)
            load(mask_t_sb[:], mask_t, mask_in)
            load(ctx_sb[:, 1, :], ctx_t[:, tok(1)], ctx_in[1])
            for i in range(3):
                load(row[:, i, :], rows[i:i + 1, :].broadcast_to([P, C]), row_in)
            for g in range(2, G):
                load(x_sb[:, grp(g), :], x_tok[:, grp(g), :], x_in[g])
            load(wexp_sb[:], w_exp_t, ffn_in)
            load(wcon_sb[:], w_con, ffn_in)
            load(local_w[:, 0, 0:n_local], up_local, ffn_in)
            load(local_w[:, 1, 0:n_local], down_local, ffn_in)
            load(cross_w[:, 0, :], up_cross, ffn_in)
            load(cross_w[:, 1, :], down_cross, ffn_in)

            def load_ctx(g):
                sp.wait_ge(kc_ok, g - 1)
                sp.wait_ge(vc_ok, g - 1)
                load(ctx_sb[:, g % 2, :], ctx_t[:, tok(g)], ctx_in[g])

            def spill_parts(s, g):
                sp.wait_ge([q_third, k_third][s], g + 1)
                sp.dma_start(spill[s][g].rearrange("n p t -> p n t"), part[s][:, g % 2, :, :]).then_inc(spilled[s][g], 16)

            def stack_rows(s, g):
                if g >= 2:
                    sp.wait_ge(s2_ok, NQ * GB * (g - 1))
                    if s == 0:
                        sp.dma_start(stack[0][SHIFT_ROW:SHIFT_ROW + NS, g % 2, :, :],
                                     stack[0][SK - NS:SK, g % 2, :, :]).then_inc(stack_zero[g % 2], 16)
                sp.wait_ge(spilled[s][g], 16)
                sp.wait_ge(stack_filled[s], 1)
                for n, count in RUNS:
                    part_n = PAIRS[n][s]
                    if s == 0:
                        src = spill[s][g, part_n:part_n + 1].to_broadcast([count, P, GT])
                    else:
                        src = spill[s][g, part_n:part_n + count]
                    sp.dma_start(stack[s][n * D:(n + count) * D, g % 2, :, :],
                                 src.rearrange("n (d h) t -> n d h t", d=D)).then_inc(stack_in[s][g % 2], 16)

            def shift_rows(b):
                g, t = divmod(b, GB)
                sp.wait_ge(shiftt_sb, b + 1)
                sp.dma_start(stack[0][SHIFT_ROW:SHIFT_ROW + NS, g % 2, :, t * T:(t + 1) * T],
                             shift_t[:, b % 2, :]).then_inc(shift_in[b % 2], 16)

            def pad_rows(s):
                sp.wait_ge(stack_filled[s], 1)
                sp.dma_start(stack[s][SHIFT_ROW:SK, 1, :, :], stack[s][SHIFT_ROW:SK, 0, :, :]).then_inc(pad_in[s], 16)

            load_ctx(2)
            spill_parts(1, 0)
            load_ctx(3)
            pad_rows(1)
            stack_rows(1, 0)
            pad_rows(0)
            spill_parts(1, 1)
            stack_rows(1, 1)
            spill_parts(1, 2)
            spill_parts(0, 0)
            stack_rows(0, 0)
            spill_parts(1, 3)
            spill_parts(0, 1)
            shift_rows(0)
            stack_rows(0, 1)
            for b in range(1, B):
                if b + 1 < G:
                    spill_parts(0, b + 1)
                shift_rows(b)
                if b % GB == 1 and b >= GB and b // GB + 1 < G:
                    stack_rows(1, b // GB + 1)
                    stack_rows(0, b // GB + 1)
            out_tok = out.rearrange("b t c -> t b c")
            for n in range(NP):
                sp.wait_ge(z3_ok, n + 1)
                sp.dma_start(out_tok[:, pair(n), :], z[:, pair(n), :]).then_inc(out_done, 16)
            sp.wait_ge(out_done, 16 * NP)

        @block.gpsimd
        def _(pool):
            chain = [0]

            def link(ins):
                chain[0] += 1
                ins.then_inc(pool_own, 1)
                pool.wait_ge(pool_own, chain[0])

            nc.gpsimd.memset(ident[:], 0.0).then_inc(ident_0, 1)
            nc.gpsimd.memset(ident_bf[:], 0.0).then_inc(ident_0, 1)
            pool.wait_ge(ident_0, 2)
            for m in (ident, ident_bf):
                nc.gpsimd.affine_select(out=m[:], in_=m[:], compare_op=ALU.not_equal, fill=1.0, base=0,
                                        pattern=[[-1, P]], channel_multiplier=1).then_inc(ident_ok, 1)
            nc.gpsimd.memset(xn[:, :, :, 0:1], 0.0).then_inc(const_ok, 1)
            nc.gpsimd.memset(neg_half[:], -0.5).then_inc(const_ok, 1)
            nc.gpsimd.memset(one_col[:], 1.0).then_inc(const_ok, 1)
            pool.wait_ge(const_ok, 3)

            def rstd_of(k, bs, last):
                n = bs.stop - bs.start
                r, m = rstd[:, k, bs], nmr[:, k, bs]
                link(nc.gpsimd.tensor_scalar(r, mv[:, bs, 1], EPS, None, ALU.add))
                link(nc.gpsimd.tensor_tensor(r, r, neg_half[:, 0:n], ALU.pow))
                link(nc.gpsimd.tensor_tensor(m, mv[:, bs, 0], r, ALU.mult))
                nc.gpsimd.tensor_scalar(m, m, -1.0, 0.0, ALU.mult, ALU.add).then_inc(last, 1)

            def gate(g):
                pool.wait_ge(num_ok, g + 1)
                if g >= 2:
                    pool.wait_ge(y_ok, g - 1)
                nc.gpsimd.tensor_tensor(gated[:, g % 2, :], num, den, ALU.mult).then_inc(gated_ok, 1)

            def third_part(s, g, rest_s, second, third):
                pool.wait_ge(second, g + 1)
                nc.gpsimd.tensor_tensor(part[s][:, g % 2, 2, :], rest[:, s, :], part[s][:, g % 2, 1, :],
                                        ALU.subtract).then_inc(third, 1)

            def add_row(g, r, done):
                nc.gpsimd.tensor_tensor(xres[:, grp(g), :], z[:, grp(g), :],
                                        r.to_broadcast([P, GB, C]), ALU.add).then_inc(done, 1)

            def stack_fill(s, half):
                two_ones = 1.0 + 0x3F80 * 2.0 ** -23
                nc.gpsimd.memset(stack[s][0:SK, half, :, :].rearrange("p h t -> p (h t)").bitcast(FP32),
                                 two_ones if s == 1 else 0.0).then_inc(stack_filled[s], 1)

            def local_up():
                pool.wait_ge(ffn_in, 96)
                at = 0
                for k in range(LOCAL):
                    n = 2 ** k
                    w = local_w[:, 0, at:at + 2 * n * FB].rearrange("p (f o j) -> p f o j", f=FB, o=2)
                    dst = local_m[0][k % 2][:, 0:2 * n * FB].rearrange("p (f o j) -> p f o j", f=FB, o=2)
                    src = local_m[0][(k + 1) % 2][:, 0:n * FB].rearrange("p (f j) -> p f j", f=FB)
                    for o in range(2):
                        if k == 0:
                            ins = nc.gpsimd.tensor_copy(dst[:, :, o, :], w[:, :, o, :])
                        else:
                            ins = nc.gpsimd.tensor_tensor(dst[:, :, o, :], w[:, :, o, :], src, ALU.mult)
                        if k == LOCAL - 1:
                            ins.then_inc(local_ok, 1)
                        else:
                            link(ins)
                    at += 2 * n * FB

            def local_down():
                at = 0
                for k in range(LOCAL - 1, -1, -1):
                    n = 2 ** (LOCAL - 1 - k)
                    w = local_w[:, 1, at:at + 2 * n * FB].rearrange("p (f i) -> p f i", i=2)
                    dst = local_m[1][k % 2][:, 0:2 * n * FB].rearrange("p (f i) -> p f i", i=2)
                    src = local_m[1][(k + 1) % 2][:, 0:n * FB]
                    for i in range(2):
                        if k == LOCAL - 1:
                            ins = nc.gpsimd.tensor_copy(dst[:, :, i], w[:, :, i])
                        else:
                            ins = nc.gpsimd.tensor_tensor(dst[:, :, i], w[:, :, i], src, ALU.mult)
                        if k == 0:
                            ins.then_inc(local_ok, 1)
                        else:
                            link(ins)
                    at += 2 * n * FB

            for s in range(-1, G + 4):
                if 0 <= s + 1 < G:
                    pool.wait_ge(stats_ok, s + 2)
                    rstd_of(0, grp(s + 1), rstd_ok)
                if 0 <= s - 4 < G:
                    third_part(0, s - 4, q_rest, q_second, q_third)
                if 0 <= s - 1 < G:
                    third_part(1, s - 1, k_rest, k_second, k_third)
                    gate(s - 1)
                if 0 <= s - 2 < G:
                    pool.wait_ge(stats1_ok, s - 1)
                    rstd_of(1, grp(s - 2), rstd1_ok)
                if s == 0:
                    stack_fill(1, 0)
                    stack_fill(0, 0)
                    local_up()
                if 0 <= s - 3 < G:
                    pool.wait_ge(z1_ok, GB * (s - 2))
                    if s == 3:
                        pool.wait_ge(row_in, 48)
                    add_row(s - 3, row[:, 0:1, :], xres1_ok)
            local_down()

            def cross(side, src, stage, dst, last):
                s = 2 ** stage
                n = src.shape[-1]
                other = hidden[0][:].rearrange("p f t -> p (f t)")[:, 0:FB * n].rearrange("p (f c) -> p f c", f=FB)
                for b in range(FB):
                    bit = (b >> stage) & 1
                    lo, hi = b & ~s, b | s
                    pair = (b >> 1) if stage == 0 else (b & 1)
                    c0 = 8 * stage + 4 * pair + (2 * bit if side == 0 else bit)
                    c1 = c0 + (1 if side == 0 else 2)
                    nc.gpsimd.tensor_scalar(dst[:, b, :], src[:, lo, :], cross_w[:, side, c0:c0 + 1], 0.0,
                                            ALU.mult, ALU.add).then_inc(pool_own, 1)
                    nc.gpsimd.tensor_scalar(other[:, b, :], src[:, hi, :], cross_w[:, side, c1:c1 + 1], 0.0,
                                            ALU.mult, ALU.add).then_inc(pool_own, 1)
                    chain[0] += 2
                pool.wait_ge(pool_own, chain[0])
                ins = nc.gpsimd.tensor_tensor(dst, dst, other, ALU.add)
                if last is not None:
                    ins.then_inc(last, 1)
                    pool.wait_ge(last, 1)
                else:
                    link(ins)

            pool.wait_ge(local_ok, 4)
            cross(1, wcon_sb, 1, down_cross_m[:, 0], None)
            cross(1, down_cross_m[:, 0], 0, down_cross_m[:, 1], downc_ok)
            pool.wait_ge(uplocal_sb, 2)
            cross(0, up_rows, 0, up_cross_m[:, 0], None)
            pool.wait_ge(stats2_ok, 1)
            rstd_of(2, slice(0, 1), rstd2_ok)
            cross(0, up_cross_m[:, 0], 1, up_cross_m[:, 1], upc_ok)
            link(nc.gpsimd.tensor_tensor(row_ffn[:], row[:, 1, :], row[:, 2, :], ALU.add))
            for b in range(1, B):
                pool.wait_ge(stats2_ok, b + 1)
                rstd_of(2, slice(b, b + 1), rstd2_ok)
                if b % GB == GB - 1:
                    pool.wait_ge(z2_ok, b + 1)
                    add_row(b // GB, row_ffn[:, None, :], xres2_ok)
                for n in [n for n, (s, q) in enumerate(RES_AT) if s - 5 == b or (b == B - 1 and s - 5 > b)]:
                    pool.wait_ge(stats3_ok, n + 1)
                    rstd_of(3, pair(n), rstd3_ok)
            for n in range(len(RES_AT), NP):
                pool.wait_ge(stats3_ok, n + 1)
                rstd_of(3, pair(n), rstd3_ok)

        @block.vector
        def _(dve):
            chain = [0]

            def link(ins):
                chain[0] += 1
                ins.then_inc(dve_own, 1)
                dve.wait_ge(dve_own, chain[0])

            def norm_stats(src, bs, done):
                for b in range(bs.start, bs.stop):
                    ins = nc.vector.bn_stats(stats[:, b, :], src[:, b, :])
                    ins.then_inc(dve_own, 1)
                    chain[0] += 1
                dve.wait_ge(dve_own, chain[0])
                for b in range(bs.start, bs.stop):
                    ins = nc.vector.bn_aggr(mv[:, b, :], stats[:, b, :])
                    if b < bs.stop - 1:
                        ins.then_inc(dve_own, 1)
                        chain[0] += 1
                dve.wait_ge(dve_own, chain[0])
                ins.then_inc(done, 1)

            nc.vector.memset(v_sb[:, :, :, D:VW], 1.0).then_inc(dve_const, 1)
            nc.vector.memset(decay_row[:], 1.0).then_inc(dve_const, 1)
            dve.wait_ge(dve_const, 2)

            def scale_weights():
                dve.wait_ge(col_in, 16)
                dve.wait_ge(w_in, 16)
                link(nc.vector.tensor_scalar(one_less[:], col[:, C_MIXK:C_MIXK + 3], -1.0, 1.0, ALU.mult, ALU.add))
                for n in range(3):
                    link(nc.vector.tensor_scalar(w_cur[:, n, :], w_sb[:, n, :], col[:, C_MIXK + n:C_MIXK + n + 1], None,
                                                 ALU.mult))
                    ins = nc.vector.tensor_scalar(w_last[:, n, :], w_sb[:, n, :], one_less[:, n:n + 1], None, ALU.mult)
                    if n < 2:
                        link(ins)
                ins.then_inc(mixw_ok, 1)

            def wkv(g):
                e = g % 2
                if g == 0:
                    dve.wait_ge(decay_ok, 1)
                    link(nc.vector.tensor_scalar(decay_row[:], decay_row[:], decay[:, 0:1], None, ALU.mult))
                    link(nc.vector.memset(decay_row[:, :, 0:1], 0.0))
                dr = decay_row[:].rearrange("p b t -> p (b t)")
                dve.wait_ge(ek_ok, g + 1)
                dve.wait_ge(proj_ok, 3 * g + 2)
                if g >= 1:
                    dve.wait_ge(gated_ok, g)
                nc.vector.tensor_tensor(ekv, ek[:, e, :], bank[2][:], ALU.mult).then_inc(ekv_ok, 1)
                link(nc.vector.tensor_tensor_scan(den, dr, ek[:, e, :], 0.0, ALU.mult, ALU.add))
                dve.wait_ge(ekv_ok, g + 1)
                link(nc.vector.tensor_tensor_scan(num, dr, ekv, 0.0, ALU.mult, ALU.add))
                dve.wait_ge(er_ok, g + 1)
                link(nc.vector.scalar_tensor_tensor(den, den, DEN_EPS, er[:, e, :], ALU.add, ALU.mult))
                nc.vector.reciprocal(den, den).then_inc(num_ok, 1)

            def split(s, g, psum, scale, first, rest_s, third):
                p, r = part[s][:, g % 2], rest[:, s, :]
                dve.wait_ge(first, g + 1)
                if g >= 1:
                    dve.wait_ge(third, g)
                nc.vector.scalar_tensor_tensor(r, psum, scale, p[:, 0, :], ALU.mult,
                                               ALU.subtract).then_inc(rest_s, 1)

            def residual1(g):
                dve.wait_ge(y_ok, g + 1)
                nc.vector.tensor_tensor(x_sb[:, grp(g), :], x_sb[:, grp(g), :],
                                        bank[4][:].rearrange("p (b c) -> p b c", b=GB), ALU.add).then_inc(res1_ok, 1)
                dve.wait_ge(res1_ok, g + 1)
                norm_stats(x_sb, grp(g), stats1_ok)

            def mixing_step(s):
                if 0 <= s - 4 < G:
                    dve.wait_ge(q_ok, s - 3)
                    split(0, s - 4, bank[6][:], QK_SCALE, q_first, q_rest, q_third)
                if 0 <= s - 1 < G:
                    wkv(s - 1)
                if 0 <= s - 2 < G:
                    residual1(s - 2)
                if 0 <= s + 2 < G:
                    dve.wait_ge(x_in[s + 2], 16)
                    norm_stats(x_sb, grp(s + 2), stats_ok)
                if s == -2:
                    scale_weights()
                if 0 <= s < G:
                    dve.wait_ge(kc_ok, s + 1)
                    split(1, s, bank[7][:], 1.0, k_first, k_rest, k_third)
                if s == 0:
                    dve.wait_ge(mask_in, 32)
                    for m, b in ((mask_sb, bias_q), (mask_t_sb, bias_k)):
                        link(nc.vector.tensor_scalar(m[:], m[:], -1.0, 1.0, ALU.mult, ALU.add))
                        link(nc.vector.tensor_scalar(b[:], m[:], MASKED, None, ALU.mult))
                    link(nc.vector.tensor_reduce(bias_top[:], bias_q[:], AX.X, ALU.max))
                    nc.vector.tensor_scalar(bias_rel[:], bias_q[:], bias_top[:, 0:1], None,
                                            ALU.subtract).then_inc(bias_ok, 1)
                    link(nc.vector.tensor_copy(bias_part[:, 0, :], bias_k[:]))
                    link(nc.vector.tensor_tensor(bias_rest[:], bias_k[:], bias_part[:, 0, :], ALU.subtract))
                    link(nc.vector.tensor_copy(bias_part[:, 1, :], bias_rest[:]))
                    nc.vector.tensor_tensor(bias_part[:, 2, :], bias_rest[:], bias_part[:, 1, :],
                                            ALU.subtract).then_inc(bias_ok, 1)

            def quad_max(b, q):
                dve.wait_ge(s1_ok, NQ * b + q + 1)
                if q == 0 and b >= 2:
                    dve.wait_ge(shift_ok, b - 1)
                nc.vector.tensor_reduce(top[:, b % 2, q * HQ:(q + 1) * HQ], quads(bank[q % 2][:]), AX.X, ALU.max,
                                        negate=True).then_inc(max_ok, 1)

            def shift_part(b, i):
                t = top[:, b % 2, :]
                if i == 0:
                    dve.wait_ge(max_ok, NQ * (b + 1))
                    if b >= 1:
                        dve.wait_ge(shiftt_ok, b)
                    nc.vector.tensor_scalar(shift[:, 0, :], t, bias_top[:, 0:1], None,
                                            ALU.subtract).then_inc(shift_step, 1)
                    return
                dve.wait_ge(shift_step, 3 * b + i)
                if i == 1:
                    if b >= 1:
                        dve.wait_ge(shift_ok, b)
                    nc.vector.scalar_tensor_tensor(top_rest[:], t, bias_top[:, 0:1], shift[:, 0, :], ALU.subtract,
                                                   ALU.subtract).then_inc(shift_step, 1)
                elif i == 2:
                    nc.vector.tensor_copy(shift[:, 1, :], top_rest[:]).then_inc(shift_step, 1)
                else:
                    nc.vector.tensor_tensor(shift[:, 2, :], top_rest[:], shift[:, 1, :],
                                            ALU.subtract).then_inc(shift_ok, 1)

            def add_bias(b, q):
                dve.wait_ge(s2_ok, NQ * b + q + 1)
                if b >= 2:
                    dve.wait_ge(av_ok, b - 1)
                nc.vector.tensor_tensor(probs[:, b % 2, q * HQ:(q + 1) * HQ, :], quads(bank[2 + q % 2][:]),
                                        bias_k[:, None, :].to_broadcast([P, HQ, T]), ALU.add).then_inc(added_ok, 1)

            def invert_sums(b):
                dve.wait_ge(ox_ok, b + 1)
                if b >= 1:
                    dve.wait_ge(norm_ok, b)
                o = bank[6][:].rearrange("p (h r) -> p h r", r=STRIP)
                nc.vector.reciprocal(rden.rearrange("p (h o) -> p h o", o=1), o[:, :, D:D + 1]).then_inc(rden_ok, 1)

            def normalise(b):
                dve.wait_ge(rden_ok, b + 1)
                if b >= 1:
                    dve.wait_ge(nt_ok, b)
                o = bank[6][:].rearrange("p (h r) -> p h r", r=STRIP)
                nc.vector.tensor_tensor(o_norm[:], o[:, :, 0:D],
                                        rden.rearrange("p (h o) -> p h o", o=1).to_broadcast([P, H, D]),
                                        ALU.mult).then_inc(norm_ok, 1)

            def residual2(b):
                dve.wait_ge(op_ok, b + 1)
                if b == 0:
                    dve.wait_ge(xres1_ok, G)
                nc.vector.tensor_tensor(x_sb[:, b, :], xres[:, b, :], bank[6][:, 0:C], ALU.add).then_inc(res2_ok, 1)

            def row_stats2(b):
                dve.wait_ge(res2_ok, b + 1)
                nc.vector.bn_stats(stats[:, b, :], x_sb[:, b, :]).then_inc(row_stats_ok, 1)

            def mean_var2(b):
                dve.wait_ge(row_stats_ok, b + 1)
                nc.vector.bn_aggr(mv[:, b, :], stats[:, b, :]).then_inc(stats2_ok, 1)

            def residual3(n):
                dve.wait_ge(f_ok, n + 1)
                dve.wait_ge(xres2_ok, n // 2 + 1)
                bs = pair(n)
                nc.vector.tensor_tensor(x_sb[:, bs, :], xres[:, bs, :],
                                        bank[5][:, 0:2 * C].rearrange("p (b c) -> p b c", b=2),
                                        ALU.add).then_inc(res3_ok, 1)
                dve.wait_ge(res3_ok, n + 1)
                norm_stats(x_sb, bs, stats3_ok)

            def output_rows(n):
                dve.wait_ge(rstd3_ok, n + 1)
                dve.wait_ge(t2_ok, 2 * n + 2)
                for b in (2 * n, 2 * n + 1):
                    ins = nc.vector.tensor_scalar(z[:, b, :], x_sb[:, b, :], rstd[:, 3, b:b + 1], nmr[:, 3, b:b + 1],
                                                  ALU.mult, ALU.add)
                    if b == 2 * n:
                        link(ins)
                ins.then_inc(z3_ok, 1)

            def attention_step(s):
                for q in range(NQ):
                    if s < B:
                        quad_max(s, q)
                    if q == 1 and 0 <= s - 5 < B:
                        row_stats2(s - 5)
                    if q == 2 and 0 <= s - 4 < B:
                        invert_sums(s - 4)
                    if 0 <= s - 2 < B and not bias_on_pe(s - 2, q):
                        add_bias(s - 2, q)
                    if q == 0 and 0 <= s - 5 < B:
                        residual2(s - 5)
                    if q == 1 and 0 <= s - 5 < B:
                        mean_var2(s - 5)
                    if q == 2 and 0 <= s - 4 < B:
                        normalise(s - 4)
                    if q == 3:
                        if s < B:
                            shift_part(s, 0)
                        if s < B:
                            shift_part(s, 1)
                            shift_part(s, 2)
                            shift_part(s, 3)
                    if (s, q) in RES_AT:
                        residual3(RES_AT[s, q])
                    if (s, q) in ROWS_AT:
                        output_rows(ROWS_AT[s, q])
                if s == DOWN_AT:
                    dve.wait_ge(upc_ok, 1)
                    nc.vector.tensor_tensor(up_b[:], up_cross_m[:, 1, :, C], col[:, C_UPB:C_UPB + FB],
                                            ALU.add).then_inc(upb_sb, 1)

            for s in range(-2, G + 1):
                mixing_step(s)
            for s in range(B + 6):
                if s < 3:
                    mixing_step(G + 1 + s)
                attention_step(s)
            for n in range(len(RES_AT), NP):
                residual3(n)
                output_rows(n)

        @block.scalar
        def _(act):
            act.wait_ge(col_in, 16)
            nc.scalar.activation(decay[:], col[:, C_DECAY:C_DECAY + 1], ACT.Exp).then_inc(decay_ok, 1)

            def apply_norm(k, bs, ready, n, done):
                act.wait_ge(ready, n)
                for b in range(bs.start, bs.stop):
                    nc.scalar.activation(z[:, b, :], x_sb[:, b, :], ACT.Identity, bias=nmr[:, k, b:b + 1],
                                         scale=rstd[:, k, b:b + 1]).then_inc(done, 1)

            def second_part(s, g, rest_s, done):
                act.wait_ge(rest_s, g + 1)
                nc.scalar.activation(part[s][:, g % 2, 1, :], rest[:, s, :], ACT.Copy).then_inc(done, 1)

            def mixing_step(s):
                if 0 <= s < G:
                    act.wait_ge(t0_ok, s + 1)
                    if s == 0:
                        act.wait_ge(const_ok, 3)
                    if s >= 2:
                        act.wait_ge(proj_ok, 3 * (s - 1))
                    nc.scalar.activation(xn[:, s % 2, :, 1:T + 1], bank[0][:].rearrange("p (b t) -> p b t", b=GB),
                                         ACT.Identity, bias=col[:, C_B:C_B + 1],
                                         scale=col[:, C_G:C_G + 1]).then_inc(xn_ok, 1)
                if 0 <= s < G:
                    act.wait_ge(vc_ok, s + 1)
                    if s == 0:
                        act.wait_ge(dve_const, 2)
                    nc.scalar.activation(v_sb[:, grp(s), :, 0:D],
                                         bank[5][:].rearrange("p (b h d) -> p b h d", b=GB, h=H),
                                         ACT.Copy).then_inc(v_ok, 1)
                if 0 <= s - 4 < G:
                    second_part(0, s - 4, q_rest, q_second)
                if 0 <= s + 1 < G:
                    apply_norm(0, grp(s + 1), rstd_ok, s + 2, z0_ok)
                if 0 <= s - 3 < G:
                    apply_norm(1, grp(s - 3), rstd1_ok, s - 2, z1_ok)
                if 0 <= s - 1 < G:
                    second_part(1, s - 1, k_rest, k_second)
                if 0 <= s < G:
                    act.wait_ge(proj_ok, 3 * s + 1)
                    if s >= 2:
                        act.wait_ge(gated_ok, s - 1)
                    nc.scalar.activation(ek[:, s % 2, :], bank[1][:], ACT.Exp).then_inc(ek_ok, 1)
                    act.wait_ge(proj_ok, 3 * s + 3)
                    nc.scalar.activation(er[:, s % 2, :], bank[3][:], ACT.Exp, scale=-1.0).then_inc(er_raw, 1)
                if 0 <= s - 3 < G:
                    act.wait_ge(t1_ok, s - 2)
                    nc.scalar.activation(zt[:, (s - 3) % 2, :], bank[5][:], ACT.Copy).then_inc(zt1_ok, 1)
                if 0 <= s < G:
                    act.wait_ge(er_raw, s + 1)
                    nc.scalar.activation(er[:, s % 2, :], er[:, s % 2, :], ACT.Identity,
                                         bias=one_col[:, 0:1]).then_inc(er_ok, 1)
                    act.wait_ge(kc_ok, s + 1)
                    if s >= 2:
                        act.wait_ge(spilled[1][s - 2], 16)
                    nc.scalar.activation(part[1][:, s % 2, 0, :], bank[7][:], ACT.Copy).then_inc(k_first, 1)
                if 0 <= s - 3 < G:
                    g = s - 3
                    act.wait_ge(q_ok, g + 1)
                    if g >= 2:
                        act.wait_ge(spilled[0][g - 2], 16)
                    nc.scalar.activation(part[0][:, g % 2, 0, :], bank[6][:], ACT.Copy,
                                         scale=QK_SCALE).then_inc(q_first, 1)

            def exps(b, q):
                p = probs[:, b % 2, q * HQ:(q + 1) * HQ, :]
                if bias_on_pe(b, q):
                    act.wait_ge(s2_ok, NQ * b + q + 1)
                    if b >= 2:
                        act.wait_ge(av_ok, b - 1)
                    src = quads(bank[2 + q % 2][:])
                else:
                    act.wait_ge(added_ok, added_before(b, q) + 1)
                    src = p
                nc.scalar.activation(p, src, ACT.Exp).then_inc(exp_ok, 1)

            def shift_copy(b):
                act.wait_ge(shiftt_ok, b + 1)
                if b >= 2:
                    act.wait_ge(shift_in[b % 2], 16 * (b // 2))
                nc.scalar.activation(shift_t[:, b % 2, :], bank[7][0:NS * H, 0:T // 2].bitcast(BF16),
                                     ACT.Copy).then_inc(shiftt_sb, 1)

            def copy_out(ready, n, dst, src, done):
                act.wait_ge(ready, n)
                nc.scalar.activation(dst, src, ACT.Copy).then_inc(done, 1)

            def hidden_copy(g, f):
                act.wait_ge(h_ok, FB * g + f + 1)
                if f == 0:
                    act.wait_ge(upb_sb, 1)
                nc.scalar.activation(hidden[g][:, f, :], bank[5][:], ACT.Identity,
                                     bias=up_b[:, f:f + 1]).then_inc(h_sb, 1)

            def gelus(g, tokens):
                t0, t1 = tokens
                for f in range(FB):
                    act.wait_ge(h_ok, FB * (g + (t0 > 0)) + f + 1)
                    if f == 0:
                        act.wait_ge(f_ok, 2 * (g - 2) + t1 * 2 // GT)
                    nc.scalar.activation(hidden[g % 2][:, f, t0:t1], bank[f][:, t0:t1], ACT.Gelu,
                                         bias=up_b[:, f:f + 1]).then_inc(gelu_ok, 1)

            def attention_step(s):
                for q in range(NQ):
                    if q == 0 and 0 <= s - 4 < B:
                        act.wait_ge(av_ok, s - 3)
                        if s - 4 >= 1:
                            act.wait_ge(ox_ok, s - 4)
                        nc.scalar.activation(o_t[:].rearrange("p g t -> p (g t)"), bank[4][:],
                                             ACT.Copy).then_inc(ot_ok, 1)
                    if q == 1 and 0 <= s - 1 < B:
                        shift_copy(s - 1)
                    if 0 <= s - 2 < B:
                        exps(s - 2, q)
                    if q == 1 and s == UP_AT:
                        act.wait_ge(y_ok, G)
                        copy_out(uplocal_ok, 1, up_rows[:, :, 0:C], bank[5][:].rearrange("p (f c) -> p f c", f=FB),
                                 uplocal_sb)
                    if q == 3 and s == UP_AT:
                        copy_out(uplocal_ok, 2, up_rows[:, :, C], bank[5][:, 0:FB], uplocal_sb)
                    if q == 1 and s == DOWN_AT:
                        copy_out(downm_ok, 1, down_m.rearrange("p f c -> p (f c)"), bank[5][:], downm_sb)
                    if q == 3 and s == DOWN_AT:
                        copy_out(upt_ok, 1, up_m.rearrange("p f c -> p (f c)"), bank[5][:], upm_ok)
                    if q == 2 and 0 <= s - 6 < B:
                        b = s - 6
                        if b >= 2 * GB:
                            act.wait_ge(h_ok, FB * (b // GB - 1))
                        copy_out(t2_ok, b + 1, zt[:, (b // GB) % 2, b % GB * T:(b % GB + 1) * T], bank[7][:, 0:T],
                                 zt2_ok)
                    if q == 3 and 0 <= s - 4 < B:
                        if s - 4 >= 1:
                            act.wait_ge(op_ok, s - 4)
                        copy_out(nt_ok, s - 3, o_norm_t[:], bank[7][:, 0:T], ntsb_ok)
                    if (s, q) in HIDDEN_AT:
                        hidden_copy(*HIDDEN_AT[s, q])
                    if (s, q) in GELU_AT:
                        g = GELU_AT[s, q]
                        act.wait_ge(h_sb, FB * (g + 1))
                        nc.scalar.activation(hidden[g][:], hidden[g][:], ACT.Gelu).then_inc(gelu_ok, FB)
                    if (s, q) in DIRECT_GELU_AT:
                        gelus(*DIRECT_GELU_AT[s, q])
                if 0 <= s - 5 < B:
                    apply_norm(2, slice(s - 5, s - 4), rstd2_ok, s - 4, z2_ok)
                if s == B + 5:
                    gelus(3, (GT // 2, GT))

            for s in range(-1, G + 1):
                mixing_step(s)
            mixing_step(G + 1)
            for s in range(B + 6):
                attention_step(s)
                if s in (1, 2):
                    mixing_step(G + 1 + s)

        @block.tensor
        def _(pe):
            def mm(out_, lhs, rhs, start=True, stop=True, **kw):
                return nc.tensor.matmul(out_, lhs, rhs, start=start, stop=stop, **kw)

            def transposes(dst, g):
                for t in range(GB):
                    ins = nc.tensor.transpose(dst[:, t * T:(t + 1) * T], z[:, g * GB + t, :], ident[:])
                return ins

            def project_in(g):
                pe.wait_ge(z0_ok, GB * (g + 1))
                if g >= 1:
                    pe.wait_ge(xn_ok, g)
                transposes(bank[0], g).then_inc(t0_ok, 1)
                pe.wait_ge(ctx_in[g], 16)
                if g >= 1:
                    pe.wait_ge(v_ok, g)
                if g >= 4:
                    pe.wait_ge(zt1_ok, g - 3)
                for t in range(GB):
                    ins = mm(bank[5][:, t * C:(t + 1) * C], ctx_sb[:, g % 2, t * T:(t + 1) * T], w_sb[:, X_V, :])
                ins.then_inc(vc_ok, 1)
                pe.wait_ge(xn_ok, g + 1)
                pe.wait_ge(mixw_ok, 1)
                for n, (free, w) in enumerate(((ek_ok, W_K), (ekv_ok, W_V), (er_raw, W_R))):
                    if g >= 1:
                        pe.wait_ge(free, g)
                    dst = bank[1 + n][:].rearrange("p (b t) -> p b t", b=GB)
                    mm(dst, w_cur[:, w, :], xn[:, g % 2, :, 1:T + 1], stop=False)
                    mm(dst, w_last[:, w, :], xn[:, g % 2, :, 0:T], start=False).then_inc(proj_ok, 1)

            def keys(g):
                if g >= 1:
                    pe.wait_ge(k_rest, g)
                mm(bank[7][:], w_sb[:, X_K, :], ctx_sb[:, g % 2, :]).then_inc(kc_ok, 1)

            def project_out(g):
                pe.wait_ge(gated_ok, g + 1)
                if g >= 1:
                    pe.wait_ge(res1_ok, g)
                for t in range(GB):
                    ins = mm(bank[4][:, t * C:(t + 1) * C], gated[:, g % 2, t * T:(t + 1) * T], w_sb[:, W_O, :])
                ins.then_inc(y_ok, 1)

            def turn_queries(g):
                pe.wait_ge(z1_ok, GB * (g + 1))
                pe.wait_ge(v_ok, min(g + 4, G))
                if g >= 1:
                    pe.wait_ge(zt1_ok, g)
                transposes(bank[5], g).then_inc(t1_ok, 1)

            def project_q(g):
                pe.wait_ge(zt1_ok, g + 1)
                if g >= 1:
                    pe.wait_ge(q_rest, g)
                mm(bank[6][:], w_sb[:, X_Q, :], zt[:, g % 2, :]).then_inc(q_ok, 1)

            up_l = local_m[0][(LOCAL - 1) % 2][:].rearrange("p (f j) -> p f j", f=FB)
            down_l = local_m[1][0][:].rearrange("p (f j) -> p f j", f=FB)
            pe.wait_ge(ident_ok, 2)
            pe.wait_ge(w_in, 16)

            def mixing_step(s):
                if 0 <= s < G:
                    project_in(s)
                if 0 <= s - 3 < G:
                    turn_queries(s - 3)
                if 0 <= s < G:
                    keys(s)
                if 0 <= s - 3 < G:
                    project_q(s - 3)
                if 0 <= s - 1 < G:
                    project_out(s - 1)

            def scores(b, q):
                g = b // GB
                if b % GB == 0 and q == 0:
                    for s in range(2):
                        pe.wait_ge(stack_in[s][g % 2], 16 * len(RUNS) * (g // 2 + 1))
                        if g == 1:
                            pe.wait_ge(pad_in[s], 16)
                    if g >= 2:
                        pe.wait_ge(stack_zero[g % 2], 16 * (g // 2))
                if NQ * b + q >= 2:
                    pe.wait_ge(max_ok, NQ * b + q - 1)
                mm(quads(bank[q % 2][:]), ident_bf[:], bias_rel[:, None, :].to_broadcast([P, HQ, T]), stop=False,
                   skip_group_check=True)
                for j in range(HQ):
                    h = HQ * q + j
                    ins = mm(bank[q % 2][:, j * T:(j + 1) * T], head_tok(0, b, h), head_tok(1, b, h), start=False,
                             stop=(j == HQ - 1), skip_group_check=True)
                ins.then_inc(s1_ok, 1)

            def scores_t(b, q):
                if q == 0:
                    pe.wait_ge(shift_in[b % 2], 16 * (b // 2 + 1))
                n = NQ * b + q - 2
                if n < 0:
                    pe.wait_ge((ekv_ok, er_raw)[q], G)
                elif bias_on_pe(n // NQ, n % NQ):
                    pe.wait_ge(exp_ok, n + 1)
                else:
                    pe.wait_ge(added_ok, added_before(n // NQ, n % NQ) + 1)
                if bias_on_pe(b, q):
                    for i in range(3):
                        mm(quads(bank[2 + q % 2][:]), ident_bf[:], bias_part[:, i, None, :].to_broadcast([P, HQ, T]),
                           start=(i == 0), stop=False, skip_group_check=True)
                for j in range(HQ):
                    h = HQ * q + j
                    if bias_on_pe(b, q):
                        ins = mm(bank[2 + q % 2][:, j * T:(j + 1) * T], head_tok(1, b, h), head_tok(0, b, h),
                                 start=False, stop=(j == HQ - 1), skip_group_check=True)
                    else:
                        ins = mm(bank[2 + q % 2][:, j * T:(j + 1) * T], head_tok(1, b, h), head_tok(0, b, h))
                ins.then_inc(s2_ok, 1)

            def values(b, q):
                pe.wait_ge(exp_ok, NQ * b + q + 1)
                if q == 0 and b == 0:
                    pe.wait_ge(res1_ok, G)
                if q == 0 and b >= 1:
                    pe.wait_ge(ot_ok, b)
                for j in range(HQ):
                    h = HQ * q + j
                    ins = mm(bank[4][STRIP * j:STRIP * j + VW, q * T:(q + 1) * T], v_sb[:, b, h, :],
                             probs[:, b % 2, h, :])
                if q == NQ - 1:
                    ins.then_inc(av_ok, 1)

            def hidden_part(g, f, dst, t0=0, t1=GT):
                pe.wait_ge(zt2_ok, GB * g + t1 // T)
                mm(dst[:, t0:t1], up_m[:, f, :], zt[:, g % 2, t0:t1]).then_inc(h_ok, 1)

            def ffn_out(n):
                pe.wait_ge(gelu_ok, FB * (n // 2 + 1 + (n == NP - 1)))
                if n >= 1:
                    pe.wait_ge(res3_ok, n)
                for t in range(2):
                    at = (n % 2 * 2 + t) * T
                    for f in range(FB):
                        ins = mm(bank[5][:, t * C:(t + 1) * C], hidden[n // 2 % 2][:, f, at:at + T], down_m[:, f, :],
                                 start=(f == 0), stop=(f == FB - 1))
                ins.then_inc(f_ok, 1)

            def beside(s, q):
                if s == UP_AT and q == 1:
                    pe.wait_ge(local_ok, 2)
                    pe.wait_ge(zt1_ok, G)
                    pe.wait_ge(v_ok, G)
                    for f in range(FB):
                        ins = mm(bank[5][:, f * C:(f + 1) * C], up_l[:, f, :], wexp_sb[:, f, 0:C])
                    ins.then_inc(uplocal_ok, 1)
                if s == UP_AT and q == 3:
                    pe.wait_ge(uplocal_sb, 1)
                    for f in range(FB):
                        ins = mm(bank[5][:, f:f + 1], up_l[:, f, :], wexp_sb[:, f, C:C + 1])
                    ins.then_inc(uplocal_ok, 1)
                if s == DOWN_AT and q == 1:
                    pe.wait_ge(uplocal_sb, 2)
                    pe.wait_ge(local_ok, 4)
                    pe.wait_ge(downc_ok, 1)
                    for f in range(FB):
                        ins = mm(bank[5][:, f * C:(f + 1) * C], down_l[:, f, :], down_cross_m[:, 1, f, :])
                    ins.then_inc(downm_ok, 1)
                if s == DOWN_AT and q == 3:
                    pe.wait_ge(downm_sb, 1)
                    pe.wait_ge(upc_ok, 1)
                    for f in range(FB):
                        ins = nc.tensor.transpose(bank[5][:, f * P:(f + 1) * P], up_cross_m[:, 1, f, 0:C], ident[:])
                    ins.then_inc(upt_ok, 1)
                if (s, q) in HIDDEN_AT:
                    g, f = HIDDEN_AT[s, q]
                    if f == 0 and g == 0:
                        pe.wait_ge(upm_ok, 1)
                    elif f == 0:
                        pe.wait_ge(res3_ok, 2 * g)
                    else:
                        pe.wait_ge(h_sb, FB * g + f)
                    hidden_part(g, f, bank[5])
                if (s, q) in DIRECT_AT:
                    g, blocks, (t0, t1) = DIRECT_AT[s, q]
                    for f in blocks:
                        if g == 2:
                            pe.wait_ge((max_ok, exp_ok)[f // 2], NQ * B)
                        else:
                            pe.wait_ge(gelu_ok, FB * 2 + f + 1)
                        hidden_part(g, f, bank[f], t0, t1)
                if (s, q) in OUT_AT:
                    ffn_out(OUT_AT[s, q])

            def attention_step(s):
                for q in range(NQ):
                    if s < B:
                        scores(s, q)
                    if q == 0 and 0 <= s - 5 < B:
                        pe.wait_ge(ntsb_ok, s - 4)
                        pe.wait_ge(norm_ok, s - 4)
                        mm(bank[6][:, 0:C], o_norm_t[:], w_sb[:, X_O, :]).then_inc(op_ok, 1)
                    if q == 1 and 0 <= s - 4 < B:
                        pe.wait_ge(ot_ok, s - 3)
                        if s - 4 == 0:
                            pe.wait_ge(q_rest, G)
                        else:
                            pe.wait_ge(res2_ok, s - 4)
                        for n in range(NQ):
                            ins = nc.tensor.transpose(bank[6][:, n * T:(n + 1) * T], o_t[:, n, :], ident[:])
                        ins.then_inc(ox_ok, 1)
                    if q == 2 and 0 <= s - 6 < B:
                        pe.wait_ge(z2_ok, s - 5)
                        pe.wait_ge(shiftt_sb, min(s, B))
                        pe.wait_ge(ntsb_ok, min(s - 4, B))
                        nc.tensor.transpose(bank[7][:, 0:T], z[:, s - 6, :], ident[:]).then_inc(t2_ok, 1)
                    if 0 <= s - 2 < B:
                        scores_t(s - 2, q)
                    if q == 0 and 0 <= s - 1 < B:
                        pe.wait_ge(shift_ok, s)
                        if s == 1:
                            pe.wait_ge(k_rest, G)
                        if s - 5 >= 0:
                            pe.wait_ge(ntsb_ok, s - 4)
                        nc.tensor.transpose(bank[7][0:NS * H, 0:T // 2].bitcast(BF16),
                                            shift[:].rearrange("p n h -> p (n h)"), ident_bf[:]).then_inc(shiftt_ok, 1)
                    if 0 <= s - 3 < B:
                        values(s - 3, q)
                    if q == 3 and 0 <= s - 4 < B:
                        pe.wait_ge(norm_ok, s - 3)
                        pe.wait_ge(shiftt_sb, min(s, B))
                        if s - 6 >= 0:
                            pe.wait_ge(zt2_ok, s - 5)
                        nc.tensor.transpose(bank[7][:, 0:T], o_norm[:].rearrange("p h d -> p (h d)"),
                                            ident[:]).then_inc(nt_ok, 1)
                    beside(s, q)
                if s == B + 5:
                    for f in range(FB):
                        pe.wait_ge(gelu_ok, FB * 3 + f + 1)
                        hidden_part(3, f, bank[f], GT // 2, GT)
                    ffn_out(NP - 1)

            for s in range(G + 1):
                mixing_step(s)
            pe.wait_ge(bias_ok, 2)
            pe.wait_ge(dve_const, 2)
            pe.wait_ge(xn_ok, G)
            pe.wait_ge(ek_ok, G)
            for s in range(B + 6):
                attention_step(s)
                if s < 3:
                    mixing_step(G + 1 + s)


def kernel(**inputs):
    import numpy as np
    import concourse.bacc as bacc
    from concourse.bass_utils import run_bass_kernel_spmd

    def f(name):
        return np.asarray(inputs[name])

    P, FB, LOCAL = 128, 4, 7
    x = f("x")
    attn = {n: f("L0_attn_" + n) for n in ("time_decay", "time_mix_k", "time_mix_v", "time_mix_r",
                                           "Wk", "Wv", "Wr", "Wo", "ln_g", "ln_b")}

    def by_dim(w):
        return w.reshape(P, 16, 8).transpose(0, 2, 1).reshape(P, P)

    weights = np.stack([attn["Wk"].T, attn["Wv"].T, attn["Wr"].T, attn["Wo"].T,
                        by_dim(f("L0_xattn_Wq")), by_dim(f("L0_xattn_Wk")), f("L0_xattn_Wv"), f("L0_xattn_Wo")], axis=1)
    columns = np.concatenate(
        [attn[n].reshape(P, 1) for n in ("time_decay", "time_mix_k", "time_mix_v", "time_mix_r", "ln_g", "ln_b")]
        + [f("L0_ffn_up_bias").reshape(FB, P).T], axis=1)
    rows = np.stack([f("L0_xattn_bo"), f("L0_ffn_b_con"), f("L0_ffn_down_bias")])
    w_exp_t = np.concatenate([f("L0_ffn_W_exp").T.reshape(FB, P, P), f("L0_ffn_b_exp").reshape(FB, P, 1)],
                             axis=2).transpose(1, 0, 2)
    w_con = f("L0_ffn_W_con").reshape(FB, P, P).transpose(1, 0, 2)

    def up_local(w):
        p, blk = np.arange(P)[:, None, None, None], np.arange(FB)[None, :, None, None]
        parts = []
        for k in range(LOCAL):
            bit, low = np.arange(2)[None, None, :, None], np.arange(2 ** k)[None, None, None, :]
            pair = ((blk * P + p) >> (k + 1) << k) + low
            parts.append(w[k][pair, bit, (p >> k) & 1].reshape(P, -1))
        return np.concatenate(parts, axis=1)

    def down_local(w):
        p, blk = np.arange(P)[:, None, None, None], np.arange(FB)[None, :, None, None]
        parts = []
        for k in range(LOCAL - 1, -1, -1):
            n = 2 ** (LOCAL - 1 - k)
            high, bit = np.arange(n)[None, None, :, None], np.arange(2)[None, None, None, :]
            pair = ((blk * n + high) << k) + (p & (2 ** k - 1))
            parts.append(w[k][pair, (p >> k) & 1, bit].reshape(P, -1))
        return np.concatenate(parts, axis=1)

    def cross(w):
        return np.stack([w[k].reshape(2, P, 2, 2).transpose(1, 0, 2, 3) for k in (LOCAL, LOCAL + 1)],
                        axis=1).reshape(P, 16)

    up, down = f("L0_ffn_up_weights"), f("L0_ffn_down_weights")
    mask = f("mask_1x1xSxS2_fk0")[0, 0]
    arrays = {
        "x": x, "ctx_t": f("ctx_1024").transpose(2, 0, 1).reshape(P, -1), "mask": mask, "mask_t": mask.T,
        "weights": weights, "columns": columns, "rows": rows, "w_exp_t": w_exp_t, "w_con": w_con,
        "up_local": up_local(up), "down_local": down_local(down), "up_cross": cross(up), "down_cross": cross(down),
    }
    nc = bacc.Bacc("TRN2", target_bir_lowering=False, num_devices=1)
    given, args = {}, []
    for name, a in arrays.items():
        a = np.ascontiguousarray(a)
        given[f"in_{name}"] = a
        args.append(nc.dram_tensor(f"in_{name}", a.shape, mybir.dt.from_np(a.dtype), kind="ExternalInput").ap())
    args.append(nc.dram_tensor("out_y", x.shape, FP32, kind="ExternalOutput").ap())
    decoder_program(nc, *args)
    r = run_bass_kernel_spmd(nc, [given], core_ids=[0])
    return r.results[0]["out_y"]
```
